# Optimizing a Trainium2 kernel written in Bass

```python
import numpy as np
import jax
import jax.numpy as jnp

def _softmax(x, axis=-1):
    return jax.nn.softmax(x, axis=axis)

def _gelu(x):
    return jax.nn.gelu(x, approximate=True)

def _silu(x):
    return jax.nn.silu(x)

def _sigmoid(x):
    return jax.nn.sigmoid(x)

def _layernorm(x, axis=-1, eps=1e-05):
    m = jnp.mean(x, axis=axis, keepdims=True)
    v = jnp.var(x, axis=axis, keepdims=True)
    return (x - m) / jnp.sqrt(v + eps)

def _scatter_add(tgt, idx, src, axis=0):
    return tgt.at[idx].add(src)

def _segment_sum(src, seg, n):
    return jax.ops.segment_sum(src, seg, n)
kernel_name = 'mk_prb_d1_jaxref_r8_c7115a'

def setup_inputs(seed: int=0):
    np.random.seed(seed)
    _w = jnp.asarray

    def _L0_attn_setup():
        import jax, jax.numpy as jnp
        import numpy as np
        D_MODEL = 128
        NUM_HEADS = 16
        D_K = D_MODEL // NUM_HEADS
        ROPE_THETA = 10000.0

        def _apply_rope(t):
            S, dk = (t.shape[-2], t.shape[-1])
            inv_freq = 1.0 / ROPE_THETA ** (jnp.arange(0, dk, 2) / dk)
            angles = jnp.outer(jnp.arange(S), inv_freq)
            cos = jnp.repeat(jnp.cos(angles), 2, axis=-1).astype(t.dtype)
            sin = jnp.repeat(jnp.sin(angles), 2, axis=-1).astype(t.dtype)
            t_even = t[..., 0::2]
            t_odd = t[..., 1::2]
            t_rot = jnp.stack([-t_odd, t_even], axis=-1).reshape(t.shape)
            return t * cos + t_rot * sin
        key = jax.random.key(seed)
        kx, kq, kk, kv, ko = jax.random.split(key, 5)
        B, S = (4, 256)
        std = (2.0 / (D_MODEL + D_MODEL)) ** 0.5

        def w(k):
            return jax.random.truncated_normal(k, -3.0, 3.0, (D_MODEL, D_MODEL), jnp.float32) * std
        return {'x': jax.random.normal(kx, (B, S, D_MODEL), jnp.float32), 'Wq': w(kq), 'Wk': w(kk), 'Wv': w(kv), 'Wo': w(ko)}
    _L0_attn_in = _L0_attn_setup()

    def _L0_ffn_setup():
        import jax, jax.numpy as jnp
        import numpy as np
        B, T, C, E, K, CAP, H = (8, 256, 128, 8, 2, 512, 512)
        key = jax.random.key(seed)
        ks = jax.random.split(key, 6)
        s = 0.02
        return {'x': jax.random.normal(ks[0], (B, T, C), jnp.float32), 'rw1': s * jax.random.normal(ks[1], (C, H), jnp.float32), 'rb1': jnp.zeros((H,), jnp.float32), 'rw2': s * jax.random.normal(ks[2], (H, E), jnp.float32), 'rb2': jnp.zeros((E,), jnp.float32), 'ew1': s * jax.random.normal(ks[3], (E, C, H), jnp.float32), 'eb1': jnp.zeros((E, H), jnp.float32), 'ew2': s * jax.random.normal(ks[4], (E, H, C), jnp.float32), 'eb2': jnp.zeros((E, C), jnp.float32)}
    _L0_ffn_in = _L0_ffn_setup()
    _d = {'L0_attn_x': _L0_attn_in['x'], 'L0_attn_Wq': _L0_attn_in['Wq'], 'L0_attn_Wk': _L0_attn_in['Wk'], 'L0_attn_Wv': _L0_attn_in['Wv'], 'L0_attn_Wo': _L0_attn_in['Wo'], 'L0_ffn_rw1': _L0_ffn_in['rw1'], 'L0_ffn_rb1': _L0_ffn_in['rb1'], 'L0_ffn_rw2': _L0_ffn_in['rw2'], 'L0_ffn_rb2': _L0_ffn_in['rb2'], 'L0_ffn_ew1': _L0_ffn_in['ew1'], 'L0_ffn_eb1': _L0_ffn_in['eb1'], 'L0_ffn_ew2': _L0_ffn_in['ew2'], 'L0_ffn_eb2': _L0_ffn_in['eb2']}
    _x0 = _d['L0_attn_x']
    _d['L0_attn_x'] = jax.random.normal(jax.random.fold_in(jax.random.key(seed), 1), (8, 512, 128), dtype=_x0.dtype)
    del _x0
    return _d

def reference(L0_attn_x, L0_attn_Wq, L0_attn_Wk, L0_attn_Wv, L0_attn_Wo, L0_ffn_rw1, L0_ffn_rb1, L0_ffn_rw2, L0_ffn_rb2, L0_ffn_ew1, L0_ffn_eb1, L0_ffn_ew2, L0_ffn_eb2):

    def _L0_attn_ref(x, Wq, Wk, Wv, Wo):
        import jax, jax.numpy as jnp
        import numpy as np
        D_MODEL = 128
        NUM_HEADS = 16
        D_K = D_MODEL // NUM_HEADS
        ROPE_THETA = 10000.0

        def _apply_rope(t):
            S, dk = (t.shape[-2], t.shape[-1])
            inv_freq = 1.0 / ROPE_THETA ** (jnp.arange(0, dk, 2) / dk)
            angles = jnp.outer(jnp.arange(S), inv_freq)
            cos = jnp.repeat(jnp.cos(angles), 2, axis=-1).astype(t.dtype)
            sin = jnp.repeat(jnp.sin(angles), 2, axis=-1).astype(t.dtype)
            t_even = t[..., 0::2]
            t_odd = t[..., 1::2]
            t_rot = jnp.stack([-t_odd, t_even], axis=-1).reshape(t.shape)
            return t * cos + t_rot * sin
        B, S, D = x.shape
        H, dk = (NUM_HEADS, D_K)
        q = jnp.einsum('bsi,io->bso', x, Wq).reshape(B, S, H, dk).swapaxes(1, 2)
        k = jnp.einsum('bsi,io->bso', x, Wk).reshape(B, S, H, dk).swapaxes(1, 2)
        v = jnp.einsum('bsi,io->bso', x, Wv).reshape(B, S, H, dk).swapaxes(1, 2)
        q = _apply_rope(q)
        k = _apply_rope(k)
        scores = jnp.einsum('bhqd,bhkd->bhqk', q, k) / dk ** 0.5
        causal = jnp.tril(jnp.ones((S, S), dtype=bool))
        scores = jnp.where(causal, scores, -jnp.inf)
        attn = jax.nn.softmax(scores, axis=-1)
        out = jnp.einsum('bhqk,bhkd->bhqd', attn, v)
        out = out.swapaxes(1, 2).reshape(B, S, D)
        return jnp.einsum('bsi,io->bso', out, Wo)

    def _L0_ffn_ref(x, rw1, rb1, rw2, rb2, ew1, eb1, ew2, eb2):
        import jax, jax.numpy as jnp
        import numpy as np
        B, T, C, E, K, CAP, H = (8, 256, 128, 8, 2, 512, 512)
        Bx, Tx, Cx = x.shape
        N = Bx * Tx
        logits = jax.nn.relu(x @ rw1 + rb1) @ rw2 + rb2
        vals, ids = jax.lax.top_k(logits, K)
        probs = jax.nn.softmax(vals, axis=-1)
        ids_f = ids.reshape(N * K)
        probs_f = probs.reshape(N * K)
        xr = jnp.repeat(x.reshape(N, Cx), K, axis=0)
        m = jax.nn.one_hot(ids_f, E, dtype=jnp.int32)
        pos = jnp.cumsum(m, axis=0) - 1
        pos_tok = jnp.take_along_axis(pos, ids_f[:, None], axis=1)[:, 0]
        keep = (pos_tok < CAP).astype(x.dtype)
        pos_c = jnp.clip(pos_tok, 0, CAP - 1)
        disp = jnp.zeros((E, CAP, Cx), x.dtype).at[ids_f, pos_c].add(xr * keep[:, None])
        h = jax.nn.relu(jnp.einsum('enc,ech->enh', disp, ew1) + eb1[:, None, :])
        eo = jnp.einsum('enh,ehc->enc', h, ew2) + eb2[:, None, :]
        y = eo[ids_f, pos_c] * (probs_f * keep)[:, None]
        return y.reshape(Bx, Tx, K, Cx).sum(axis=2)
    x = L0_attn_x
    xn = _layernorm(x, axis=-1)
    x = x + _L0_attn_ref(xn, L0_attn_Wq, L0_attn_Wk, L0_attn_Wv, L0_attn_Wo) + _L0_ffn_ref(xn, L0_ffn_rw1, L0_ffn_rb1, L0_ffn_rw2, L0_ffn_rb2, L0_ffn_ew1, L0_ffn_eb1, L0_ffn_ew2, L0_ffn_eb2)
    return x

_drawn_inputs = setup_inputs


def setup_inputs(seed=0):
    import zlib

    import numpy as np

    out = dict(_drawn_inputs(seed))
    spreads = {'L0_ffn_rb1': (0.0, 0.1),
     'L0_ffn_rb2': (0.0, 0.1),
     'L0_ffn_eb1': (0.0, 0.719),
     'L0_ffn_eb2': (0.0, 0.1)}
    factors = {}
    for name, (base, spread) in spreads.items():
        noise = np.random.default_rng([zlib.crc32(name.encode()), seed]).standard_normal(out[name].shape)
        drawn = base * np.exp(spread * noise) if base else spread * noise
        out[name] = jnp.asarray(drawn.astype(out[name].dtype))
    for name, factor in factors.items():
        out[name] = (out[name] * factor).astype(out[name].dtype)
    return out
```

```python
from contextlib import ExitStack

import concourse.bass as bass
from concourse import mybir

F32 = mybir.dt.float32
BF16 = mybir.dt.bfloat16
U32 = mybir.dt.uint32
ALU = mybir.AluOpType
ACT = mybir.ActivationFunctionType
AXX = mybir.AxisListType.X

P = 128
HEADS = 16
PARTS = 3
TERMS = PARTS * PARTS
EPS = 1e-5
BIG = 3.0e38
FAR_SLOT = 65536.0


SPARE = {}


def at_least(eng, sem, value):
    if not isinstance(value, int) or value > 0:
        eng.wait_ge(sem, value)


def wait_first(eng, sem, value):
    eng.wait_ge(sem, value)
    if not isinstance(value, int):
        eng.sem_inc(SPARE[id(eng)], 1)


def build(nc, x, Wq, Wk, Wv, Wo, rw1, rb1, rw2, rb2, ew1, eb1, ew2, eb2,
          ident_in, cos_in, sin_in, amask_in, tri_in, sel_in, erow_in, zeros_in, out):
    B, S, C = x.shape
    E, _, H = ew1.shape
    CAP = S
    N = B * S
    NT = N // P
    TS = S // P
    HJ = H // P
    DK = C // HEADS
    QUADS = HEADS // 4
    ROWS = TERMS * DK
    MROW = ROWS
    KROWS = 96
    SCALE = float(DK) ** -0.5
    VW = 32
    assert (C, S, TS, QUADS, HJ) == (P, 512, 4, 4, 4)

    PAIR_UNITS = [[(0, 0, 0, 512)], [(0, 1, 0, 384), (0, 3, 384, 128)],
                  [(1, 0, 0, 512)], [(1, 1, 0, 384), (1, 3, 384, 128)],
                  [(0, 2, 0, 256), (1, 2, 256, 256)]]
    UNITS = [[(2 * i + h, kt, c, n) for h, kt, c, n in unit] for i in range(2) for unit in PAIR_UNITS]
    NU = len(UNITS)
    PIECE = {(h, kt): (u * 512 + c, n) for u, unit in enumerate(UNITS) for h, kt, c, n in unit}
    ATILES = [(h, qt) for h in range(4) for qt in range(TS)]
    NA = len(ATILES)

    scatter_rows = nc.dram_tensor("scatter_rows", (E * CAP, C), F32, kind="Internal").ap()
    expert_rows = nc.dram_tensor("expert_rows", (E * CAP, C), F32, kind="Internal").ap()
    qk_dram = nc.dram_tensor("qk_dram", (B * 2 * P, TERMS * S), BF16, kind="Internal").ap()
    m_dram = nc.dram_tensor("m_dram", (B * QUADS * 16, 2 * P), BF16, kind="Internal").ap()
    o_dram = nc.dram_tensor("o_dram", (B * QUADS * P, S), F32, kind="Internal").ap()
    oc_dram = nc.dram_tensor("oc_dram", (B * P, S), F32, kind="Internal").ap()
    d_dram = nc.dram_tensor("d_dram", (B * HEADS, S), F32, kind="Internal").ap()
    rb_dram = nc.dram_tensor("rb_dram", (B * P, S), F32, kind="Internal").ap()
    r_dram = nc.dram_tensor("r_dram", (B * HEADS, S), F32, kind="Internal").ap()

    with ExitStack() as ctx:
        def sb(name, shape, dt=F32):
            return ctx.enter_context(nc.sbuf_tensor(name, shape, dt))

        def sem(name):
            return ctx.enter_context(nc.semaphore(name))

        banks = [ctx.enter_context(nc.psum_tensor(f"bank{i}", [P, 512], F32)) for i in range(8)]
        bank_a = banks[0:2]
        bank_b = banks[2:4]
        bank_o = banks[4:6]
        bank_proj = banks[6]
        bank_misc = banks[7]

        ident = sb("ident", [P, P])
        cosT = sb("cosT", [P, S])
        sinT = sb("sinT", [P, S])
        amask = sb("amask", [P, S])
        tri = sb("tri", [P, P])
        ones = sb("ones", [P, P])
        sel = sb("sel", [P, E])
        erow = sb("erow", [P, 2 * E])
        wq = sb("wq", [P, C])
        wk = sb("wk", [P, C])
        wqr = sb("wqr", [P, C])
        wkr = sb("wkr", [P, C])
        wv = sb("wv", [P, C])
        wo = sb("wo", [P, C])
        w1r = sb("w1r", [P, H])
        bias_rows = sb("bias_rows", [HJ * (E + 1), P])
        biases = sb("biases", [P, HJ * (E + 1)])
        w2r = sb("w2r", [P, HJ, 32])
        b2r = sb("b2r", [P, E])
        b2s = sb("b2s", [P, C])
        res = sb("res", [P, NT * C])
        xn_all = sb("xn_all", [P, NT * C])
        xnT = sb("xnT", [P, N])
        xn = sb("xn", [P, TS, C])
        stats = sb("stats", [P, TS, 6])
        mv = sb("mv", [P, TS, 2])
        vpe = sb("vpe", [P, TS])
        nhalf = sb("nhalf", [P, TS])
        rstd = sb("rstd", [P, TS])
        hid = sb("hid", [P, HJ, S])
        lgT = sb("lgT", [P, S])
        dspT = lgT
        logits = sb("logits", [P, NT * E])
        rt = [sb(f"rt{i}", [P, NT * E]) for i in range(8)]
        rs = [sb(f"rs{i}", [P, NT]) for i in range(12)]
        slot_out = sb("slot_out", [P, 2, NT], U32)
        slot_in = sb("slot_in", [P, 2, NT], U32)
        weight = sb("weight", [P, 2, NT])
        zrow = sb("zrow", [P, S])
        w1s = sb("w1s", [P, H])
        w2s = sb("w2s", [P, HJ, C])
        dsp = sb("dsp", [P, TS, C])
        eo = sb("eo", [P, TS * C])
        rows = dsp
        xv = sb("xv", [P, S])
        rope = sb("rope", [P, 4, S])
        qk = sb("qk", [P, 2, S])
        parts = sb("parts", [P, 2, PARTS, S], BF16)
        Q = sb("Q", [P, QUADS, 4, S], BF16)
        K = sb("K", [P, QUADS, 4, S], BF16)
        rmax = sb("rmax", [P, 2, NA])
        negm = sb("negm", [16, 2, P], BF16)
        probs = sb("probs", [P, 2, NU * 512])
        vstage = sb("vstage", [P, TS, HEADS, DK])
        vaug = sb("vaug", [P, QUADS, TS, 4, VW])
        osb = sb("osb", [P, 2, S])
        oT = sb("oT", [P, S])
        dcomp = sb("dcomp", [P, 64])
        rcomp = sb("rcomp", [P, 64])
        rbc = sb("rbc", [P, S])

        s = {}
        for name in """consts_loaded weights_loaded x_loaded init_done sums_init rotated var_ready rstd_ready
            xn_ready xn_kept xnT_ready xnT_copied hid_ready hid_relu lgT_ready lgT_copied lg_ready
            logits_ready route biases_ready biases_copied scan_ready scan_copied gap_ready gap_exp slots_ready slots_zeroed scattered0 scattered1
            xv_loaded v_ready v_copied vaug_ready proj_ready rope_mul rope_sum part1 rest1 part2 part3
            qk_stored a_ready rowmax_done mt_ready negm_ready
            m_stored scores_ready exp_done probs_masked pv_done o_copied
            d_closed o_closed d_loaded o_loaded rec_ready rec_stored rec_spread rbc_loaded on_ready out_ready res_added
            ew_loaded disp_loaded dT_ready dT_copied eh_ready eh_relu eo_ready eo_copied eo_stored
            combined out_stored dve_passed pool_passed""".split():
            s[name] = sem(name)
        slot_loaded = [sem(f"slot_loaded{j}") for j in range(QUADS)]
        m_loaded = [sem(f"m_loaded{j}") for j in range(QUADS)]
        o_stored = [sem(f"o_stored{p}") for p in range(2)]
        gathered = [sem(f"gathered{i}") for i in range(4)]

        block = ctx.enter_context(nc.Block())

        CONSTS = [(ident, ident_in), (cosT, cos_in), (sinT, sin_in), (amask, amask_in), (tri, tri_in),
                  (sel, sel_in), (erow, erow_in)]
        WEIGHTS = [(wq, Wq), (wk, Wk), (wv, Wv), (wo, Wo), (w1r, rw1)]

        @block.sync
        def _(sp):
            for dst, src in CONSTS:
                sp.dma_start(dst[:], src).then_inc(s["consts_loaded"], 16)
            xt = x.rearrange("b (t p) c -> p (b t) c", p=P)
            rest = res[:].rearrange("p (t c) -> p t c", c=C)
            def load_x(b):
                at_least(sp, s["x_loaded"], 16 * b)
                sp.dma_start(rest[:, bass.ds(b * TS, TS), :], xt[:, bass.ds(b * TS, TS), :]).then_inc(s["x_loaded"], 16)

            load_x(0)
            with sp.Fori(1, B) as b:
                load_x(b)
            for dst, src in WEIGHTS:
                sp.dma_start(dst[:], src).then_inc(s["weights_loaded"], 16)
            sp.wait_ge(s["init_done"], 5)
            sp.dma_start(w2r[:, :, 0:E], rw2.rearrange("(j p) e -> p j e", p=P)).then_inc(s["weights_loaded"], 16)
            sp.dma_start(bias_rows[0:HJ, :], rb1.rearrange("(j p) -> j p", p=P)).then_inc(s["weights_loaded"], 16)
            sp.dma_start(b2r[:], rb2.rearrange("(o e) -> o e", o=1).broadcast_to([P, E])).then_inc(s["weights_loaded"], 16)
            sp.dma_start(bias_rows[HJ:, :], eb1.rearrange("e (j p) -> (e j) p", p=P)).then_inc(s["weights_loaded"], 16)
            for e in range(E):
                sp.dma_start(scatter_rows.rearrange("(e t p) c -> e p t c", p=P, t=TS)[e], zrow[:].rearrange("p (t c) -> p t c", c=C)).then_inc(s["slots_zeroed"], 16)

            def store_parts(b, w):
                sp.wait_ge(s["part3"], 2 * b + w + 1)
                dst = qk_dram[bass.ds((2 * b + w) * P, P), :].rearrange("p (i j n) -> p i j n", i=PARTS, j=PARTS)
                for r in range(PARTS):
                    sp.dma_start(dst[:, :, r, :] if w == 0 else dst[:, r, :, :], parts[:, w]).then_inc(s["qk_stored"], 16)

            def load_slot(b, j):
                sp.wait_ge(s["qk_stored"], 96 * b + 96)
                for w, dst in ((0, Q), (1, K)):
                    src = qk_dram[bass.ds((2 * b + w) * P + j * 4 * DK, 4 * DK), :].rearrange("(h d) (t n) -> (d t) h n", d=DK, t=TERMS)
                    sp.dma_start(dst[0:ROWS, j], src).then_inc(slot_loaded[j], 16)
                sp.dma_start(Q[MROW:MROW + 2, j].rearrange("p h n -> p (h n)").bitcast(F32), zeros_in).then_inc(slot_loaded[j], 16)

            def load_max(b, j):
                g = QUADS * b + j
                sp.wait_ge(s["negm_ready"], 2 * g + 2)
                md = m_dram[bass.ds(g * 16, 16), :]
                sp.dma_start(md, negm[:].rearrange("p k q -> p (k q)")).then_inc(s["m_stored"], 16)
                sp.wait_ge(s["m_stored"], 16 * g + 16)
                sp.wait_ge(s["rowmax_done"], NA * (g + 1))
                sp.dma_start(Q[MROW:MROW + 2, j].rearrange("p h (t q) -> p (h t) q", q=P),
                             md.rearrange("a (k q) -> k a q", k=2)).then_inc(m_loaded[j], 16)

            def store_o(b, j):
                g = QUADS * b + j
                sp.wait_ge(s["o_copied"], g + 1)
                sp.dma_start(o_dram[bass.ds(g * P, P), :], osb[:, j % 2, :]).then_inc(o_stored[j % 2], 16)

            def finish_gather(b):
                for p in range(2):
                    sp.wait_ge(o_stored[p], 16 * (2 * b + 2))
                od = o_dram[bass.ds(b * QUADS * P, QUADS * P), :].rearrange("(h r) n -> h r n", r=VW)
                sp.dma_start(d_dram[bass.ds(b * HEADS, HEADS), :], od[:, DK, :]).then_inc(s["d_closed"], 16)
                sp.dma_start(oc_dram[bass.ds(b * P, P), :].rearrange("(h d) n -> h d n", d=DK), od[:, 0:DK, :]).then_inc(s["o_closed"], 16)

            def finish_loads(b):
                sp.wait_ge(s["d_closed"], 16 * b + 16)
                sp.dma_start(dcomp[:], d_dram[bass.ds(b * HEADS, HEADS), :].rearrange("h (a n) -> (h a) n", n=64)).then_inc(s["d_loaded"], 16)
                sp.wait_ge(s["o_closed"], 16 * b + 16)
                if not (isinstance(b, int) and b == 0):
                    sp.wait_ge(s["out_ready"], b)
                sp.dma_start(oT[:], oc_dram[bass.ds(b * P, P), :]).then_inc(s["o_loaded"], 16)

            def store_recip(b):
                sp.wait_ge(s["rec_ready"], b + 1)
                sp.dma_start(r_dram[bass.ds(b * HEADS, HEADS), :].rearrange("h (a n) -> (h a) n", n=64), rcomp[:]).then_inc(s["rec_stored"], 16)

            def spread_recip(b):
                sp.wait_ge(s["rec_stored"], 16 * b + 16)
                src = r_dram[bass.ds(b * HEADS, HEADS), :].rearrange("h (o n) -> h o n", o=1).broadcast_to([HEADS, DK, S])
                sp.dma_start(rb_dram[bass.ds(b * P, P), :].rearrange("(h d) n -> h d n", d=DK), src).then_inc(s["rec_spread"], 16)

            def load_recip(b):
                sp.wait_ge(s["rec_spread"], 16 * b + 16)
                if not (isinstance(b, int) and b == 0):
                    sp.wait_ge(s["on_ready"], b)
                sp.dma_start(rbc[:], rb_dram[bass.ds(b * P, P), :]).then_inc(s["rbc_loaded"], 16)

            def load_xv(b, first):
                if not first:
                    sp.wait_ge(s["v_ready"], b)
                sp.dma_start(xv[:], xnT[:, bass.ds(b * S, S)]).then_inc(s["xv_loaded"], 16)

            def body(b, first, last):
                load_xv(b, first)
                if not first:
                    sp.wait_ge(s["scores_ready"], NU * QUADS * b)
                load_slot(b, 3)
                load_max(b, 1)
                if not first:
                    store_o(b - 1, 3)
                    finish_gather(b - 1)
                if not last:
                    store_parts(b + 1, 0)
                if not first:
                    finish_loads(b - 1)
                if not last:
                    store_parts(b + 1, 1)
                if not first:
                    store_recip(b - 1)
                for j in range(1, QUADS):
                    if not last:
                        sp.wait_ge(s["scores_ready"], NU * (QUADS * b + j))
                        load_slot(b + 1, j - 1)
                    if j < 3:
                        load_max(b, j + 1)
                    elif not last:
                        load_max(b + 1, 0)
                    store_o(b, j - 1)
                    if not first and j == 1:
                        spread_recip(b - 1)
                    if not first and j == 2:
                        load_recip(b - 1)

            sp.wait_ge(s["init_done"], 5)
            sp.wait_ge(s["xnT_copied"], B)
            store_parts(0, 0)
            store_parts(0, 1)
            for j in range(3):
                load_slot(0, j)
            load_max(0, 0)
            body(0, True, False)
            body(1, False, False)
            with sp.Fori(2, B - 1) as b:
                body(b, False, False)
            body(B - 1, False, True)
            store_o(B - 1, 3)
            finish_gather(B - 1)
            finish_loads(B - 1)
            store_recip(B - 1)
            spread_recip(B - 1)
            load_recip(B - 1)

            sp.wait_ge(s["scattered0"], 16 * NT)
            sp.wait_ge(s["scattered1"], 16 * NT)
            def expert(e):
                at_least(sp, s["dT_ready"], e)
                sp.dma_start(dsp[:], scatter_rows[bass.ds(e * CAP, CAP), :].rearrange("(t p) c -> p t c", p=P)).then_inc(s["disp_loaded"], 16)
                at_least(sp, s["eo_copied"], e)
                sp.dma_start(w1s[:], ew1.rearrange("e c h -> (e c) h")[bass.ds(e * C, C), :]).then_inc(s["ew_loaded"], 16)
                sp.dma_start(w2s[:], ew2.rearrange("e h c -> (e h) c")[bass.ds(e * H, H), :].rearrange("(j p) c -> p j c", p=P)).then_inc(s["ew_loaded"], 16)
                sp.dma_start(b2s[:], eb2[bass.ds(e, 1), :].broadcast_to([P, C])).then_inc(s["ew_loaded"], 16)
                at_least(sp, s["eo_copied"], e + 1)
                sp.dma_start(expert_rows[bass.ds(e * CAP, CAP), :].rearrange("(t p) c -> p t c", p=P),
                             eo[:].rearrange("p (t c) -> p t c", c=C)).then_inc(s["eo_stored"], 16)

            expert(0)
            with sp.Fori(1, E) as e:
                expert(e)
            ot = out.rearrange("b (t p) c -> p (b t) c", p=P)
            for b in range(B):
                sp.wait_ge(s["combined"], 2 * TS * (b + 1))
                sp.dma_start(ot[:, b * TS:(b + 1) * TS, :], rest[:, b * TS:(b + 1) * TS, :]).then_inc(s["out_stored"], 16)
            sp.wait_ge(s["out_stored"], 16 * B)

        @block.vector
        def _(dve):
            SPARE[id(dve)] = s["dve_passed"]
            v = nc.vector
            count = [0]

            def step(ins):
                count[0] += 1
                ins.then_inc(s["route"], 1)
                dve.wait_ge(s["route"], count[0])

            v.memset(w2r[:], 0.0).then_inc(s["init_done"], 1)
            v.memset(zrow[:], 0.0).then_inc(s["init_done"], 1)
            v.memset(Q[64:KROWS], 0.0).then_inc(s["init_done"], 1)
            v.memset(K[64:KROWS], 1.0).then_inc(s["init_done"], 1)
            v.memset(vaug[:], 1.0).then_inc(s["init_done"], 1)
            v.memset(nhalf[:], -0.5).then_inc(s["sums_init"], 1)
            v.memset(ones[:], 1.0).then_inc(s["sums_init"], 1)

            def router(b):
                at_least(dve, s["x_loaded"], 16 * b + 16)
                xs = res[:, bass.ds(b * TS * C, TS * C)].rearrange("p (t c) -> p t c", c=C)
                for t in range(TS):
                    ins = v.bn_stats(stats[:, t, :], xs[:, t, :])
                ins.then_inc(s["var_ready"], 1)
                wait_first(dve, s["var_ready"], 3 * b + 1)
                for t in range(TS):
                    ins = v.bn_aggr(mv[:, t, :], stats[:, t, :])
                ins.then_inc(s["var_ready"], 1)
                at_least(dve, s["var_ready"], 3 * b + 2)
                v.tensor_scalar(vpe[:], mv[:, :, 1], EPS, None, ALU.add).then_inc(s["var_ready"], 1)
                at_least(dve, s["rstd_ready"], b + 1)
                at_least(dve, s["xnT_ready"], b)
                at_least(dve, s["xn_kept"], b)
                for t in range(TS):
                    ins = v.tensor_scalar(xn[:, t, :], xs[:, t, :], mv[:, t, 0:1], rstd[:, t:t + 1], ALU.subtract, ALU.mult)
                ins.then_inc(s["xn_ready"], 1)
                at_least(dve, s["lg_ready"], b + 1)
                v.tensor_tensor(logits[:, bass.ds(b * TS * E, TS * E)].rearrange("p (t e) -> p t e", e=E),
                                bank_b[1][:, 0:TS * E].rearrange("p (t e) -> p t e", e=E),
                                b2r[:].rearrange("p (o e) -> p o e", o=1).broadcast_to([P, TS, E]), ALU.add).then_inc(s["logits_ready"], 1)

            router(0)
            with dve.Fori(1, B) as b:
                router(b)

            for w, wr in ((wq, wqr), (wk, wkr)):
                src = w[:].rearrange("p (i k) -> p i k", k=2)
                dst = wr[:].rearrange("p (i k) -> p i k", k=2)
                v.tensor_scalar(dst[:, :, 0], src[:, :, 1], -1.0, None, ALU.mult).then_inc(s["rotated"], 1)
                v.tensor_copy(dst[:, :, 1], src[:, :, 0]).then_inc(s["rotated"], 1)

            def ropes(b, w, k):
                i = 4 * b + 2 * w + k
                dve.wait_ge(s["proj_ready"], i + 1)
                if not (isinstance(b, int) and b == 0):
                    dve.wait_ge(s["rope_sum"], 2 * (b - 1) + w + 1)
                v.tensor_tensor(rope[:, 2 * w + k, :], bank_proj[:], (cosT if k == 0 else sinT)[:], ALU.mult).then_inc(s["rope_mul"], 1)

            def rowmax(b, j, t):
                h, qt = ATILES[t]
                g = QUADS * b + j
                n = P * (qt + 1)
                bank = bank_a[t % 2]
                if t == 0 and not (isinstance(b, int) and g < 2):
                    dve.wait_ge(s["mt_ready"], g - 1)
                wait_first(dve, s["a_ready"], NA * g + t + 1)
                v.tensor_tensor_reduce(bank[:, 0:n], bank[:, 0:n], amask[:, S - n:S], 1.0, -BIG, ALU.add, ALU.max,
                                       rmax[:, j % 2, 4 * h + qt:4 * h + qt + 1]).then_inc(s["rowmax_done"], 1)

            def neg_max(b, j):
                g = QUADS * b + j
                dve.wait_ge(s["mt_ready"], g + 1)
                if not (isinstance(b, int) and g == 0):
                    dve.wait_ge(s["m_stored"], 16 * g)
                v.tensor_scalar(negm[:, 0, :], bank_misc[0:16, 0:P], -1.0, None, ALU.mult).then_inc(s["negm_ready"], 1)
                dve.wait_ge(s["negm_ready"], 2 * g + 1)
                v.scalar_tensor_tensor(out=negm[:, 1, :], in0=bank_misc[0:16, 0:P], scalar=-1.0, in1=negm[:, 0, :],
                                       op0=ALU.mult, op1=ALU.subtract).then_inc(s["negm_ready"], 1)

            def finish_recip(b):
                dve.wait_ge(s["d_loaded"], 16 * (b + 1))
                if not (isinstance(b, int) and b == 0):
                    dve.wait_ge(s["rec_stored"], 16 * b)
                v.reciprocal(rcomp[:], dcomp[:]).then_inc(s["rec_ready"], 1)

            def finish_norm(b):
                dve.wait_ge(s["o_loaded"], 16 * (b + 1))
                dve.wait_ge(s["rbc_loaded"], 16 * (b + 1))
                if not (isinstance(b, int) and b == 0):
                    dve.wait_ge(s["out_ready"], b)
                v.tensor_tensor(oT[:], oT[:], rbc[:], ALU.mult).then_inc(s["on_ready"], 1)

            def finish_add(b):
                dve.wait_ge(s["out_ready"], b + 1)
                r = res[:, bass.ds(b * S, S)]
                v.tensor_tensor(r, bank_misc[:], r, ALU.add).then_inc(s["res_added"], 1)

            def body(b, first, last):
                for j in range(QUADS):
                    for t in range(NA):
                        if j < 2:
                            rowmax(b, j + 2, t)
                        elif not last:
                            rowmax(b + 1, j - 2, t)
                        if j == 0 and not last and t in (2, 5, 8, 11):
                            i = (t - 2) // 3
                            ropes(b + 1, i // 2, i % 2)
                        if t == 5:
                            if j < 3:
                                neg_max(b, j + 1)
                            elif not last:
                                neg_max(b + 1, 0)
                        if not first:
                            if j == 1 and t == 3:
                                finish_recip(b - 1)
                            if j == 3 and t == 2:
                                finish_norm(b - 1)
                            if j == 3 and t == 15:
                                finish_add(b - 1)

            for i in range(4):
                ropes(0, i // 2, i % 2)

            def grid(a):
                return a[:].rearrange("p (t e) -> p t e", e=E)

            def wide(a):
                return a[:].rearrange("p (t o) -> p t o", o=1).broadcast_to([P, NT, E])

            pref = erow[:, 0:E].rearrange("p (o e) -> p o e", o=1).broadcast_to([P, NT, E])
            base = erow[:, E:2 * E].rearrange("p (o e) -> p o e", o=1).broadcast_to([P, NT, E])
            dve.wait_ge(s["logits_ready"], B)
            hot = [rt[0], rt[1]]
            top = [rs[0], rs[1]]
            cur = logits
            for k in range(2):
                step(v.tensor_reduce(top[k][:], grid(cur), AXX, ALU.max))
                step(v.tensor_tensor(grid(rt[2]), grid(cur), wide(top[k]), ALU.is_equal))
                step(v.tensor_tensor(grid(rt[3]), grid(rt[2]), pref, ALU.mult))
                step(v.tensor_reduce(rs[2][:], grid(rt[3]), AXX, ALU.max))
                step(v.tensor_tensor(grid(hot[k]), grid(rt[3]), wide(rs[2]), ALU.is_equal))
                if k == 0:
                    step(v.scalar_tensor_tensor(out=grid(rt[4]), in0=grid(hot[0]), scalar=-BIG, in1=grid(logits), op0=ALU.mult, op1=ALU.add))
                    cur = rt[4]
            v.tensor_tensor(rs[3][:], top[1][:], top[0][:], ALU.subtract).then_inc(s["gap_ready"], 1)
            v.tensor_tensor(rt[5][:], hot[0][:], hot[1][:], ALU.add).then_inc(s["scan_ready"], 1)
            dve.wait_ge(s["gap_exp"], 1)
            step(v.tensor_scalar(rs[5][:], rs[4][:], 1.0, None, ALU.add))
            step(v.reciprocal(rs[6][:], rs[5][:]))
            step(v.tensor_tensor(rs[7][:], rs[4][:], rs[6][:], ALU.mult))
            dve.wait_ge(s["scan_copied"], 1)
            for e in range(E):
                ins = v.tensor_tensor_scan(grid(rt[6])[:, :, e], grid(rt[3])[:, :, e], zrow[:, 0:NT], 0.0, ALU.add, ALU.add)
            step(ins)
            step(v.tensor_tensor(rt[7][:], rt[6][:], rt[3][:], ALU.subtract))
            step(v.tensor_tensor(rt[6][:], rt[7][:], rt[2][:], ALU.add))
            for k in range(2):
                step(v.tensor_tensor(rt[3][:], rt[6][:], hot[k][:], ALU.mult))
                step(v.tensor_reduce(rs[2][:], grid(rt[3]), AXX, ALU.add))
                step(v.tensor_tensor(grid(rt[3]), grid(hot[k]), base, ALU.mult))
                step(v.tensor_reduce(rs[8][:], grid(rt[3]), AXX, ALU.add))
                step(v.tensor_scalar(rs[9][:], rs[2][:], float(CAP), None, ALU.is_le))
                step(v.tensor_tensor(weight[:, k, :], rs[9][:], rs[6 + k][:], ALU.mult))
                step(v.tensor_scalar(rs[10][:], rs[2][:], float(CAP), -1.0, ALU.min, ALU.add))
                step(v.tensor_tensor(slot_in[:, k, :], rs[10][:], rs[8][:], ALU.add))
                step(v.tensor_scalar(rs[11][:], rs[9][:], -FAR_SLOT, FAR_SLOT, ALU.mult, ALU.add))
                step(v.tensor_tensor(rs[10][:], rs[10][:], rs[8][:], ALU.add))
                v.tensor_tensor(slot_out[:, k, :], rs[10][:], rs[11][:], ALU.add).then_inc(s["slots_ready"], 1)
                dve.wait_ge(s["slots_ready"], k + 1)

            for j in range(2):
                for t in range(NA):
                    rowmax(0, j, t)
            neg_max(0, 0)
            body(0, True, False)
            body(1, False, False)
            with dve.Fori(2, B - 1) as b:
                body(b, False, False)
            body(B - 1, False, True)
            finish_recip(B - 1)
            finish_norm(B - 1)
            finish_add(B - 1)

            def expert(e):
                at_least(dve, s["eo_ready"], e + 1)
                at_least(dve, s["eo_stored"], 16 * e)
                v.tensor_tensor(eo[:].rearrange("p (t c) -> p t c", c=C), bank_o[0][:].rearrange("p (t c) -> p t c", c=C),
                                b2s[:].rearrange("p (o c) -> p o c", o=1).broadcast_to([P, TS, C]),
                                ALU.add).then_inc(s["eo_copied"], 1)

            expert(0)
            with dve.Fori(1, E) as e:
                expert(e)
            dve.wait_ge(s["res_added"], B)
            for t in range(NT):
                for k in range(2):
                    i = 2 * t + k
                    dve.wait_ge(gathered[i % 4], 16 * (i // 4 + 1))
                    if k == 1:
                        dve.wait_ge(s["combined"], i)
                    r = res[:, t * C:(t + 1) * C]
                    v.scalar_tensor_tensor(out=r, in0=rows[:, i % 4, :], scalar=weight[:, k, t:t + 1], in1=r,
                                           op0=ALU.mult, op1=ALU.add).then_inc(s["combined"], 1)

        @block.gpsimd
        def _(pool):
            SPARE[id(pool)] = s["pool_passed"]
            p = nc.gpsimd
            pool.wait_ge(s["sums_init"], 2)
            def router(b):
                at_least(pool, s["var_ready"], 3 * b + 3)
                at_least(pool, s["xn_ready"], b)
                p.tensor_tensor(rstd[:], vpe[:], nhalf[:], ALU.pow).then_inc(s["rstd_ready"], 1)
                at_least(pool, s["xn_ready"], b + 1)
                p.tensor_copy(xn_all[:, bass.ds(b * TS * C, TS * C)], xn[:].rearrange("p t c -> p (t c)")).then_inc(s["xn_kept"], 1)

            router(0)
            with pool.Fori(1, B) as b:
                router(b)

            def split(b, w, k):
                i = 2 * b + w
                if k == 0:
                    pool.wait_ge(s["rope_mul"], 2 * i + 2)
                    if not (isinstance(b, int) and b == 0):
                        pool.wait_ge(s["part3"], i - 1)
                    p.tensor_tensor(qk[:, w, :], rope[:, 2 * w, :], rope[:, 2 * w + 1, :], ALU.add).then_inc(s["rope_sum"], 1)
                elif k == 1:
                    pool.wait_ge(s["part1"], i + 1)
                    if not (isinstance(b, int) and b == 0):
                        pool.wait_ge(s["part3"], i - 1)
                    p.tensor_tensor(qk[:, w, :], qk[:, w, :], parts[:, w, 0, :], ALU.subtract).then_inc(s["rest1"], 1)
                else:
                    pool.wait_ge(s["part2"], i + 1)
                    p.tensor_tensor(parts[:, w, 2, :], qk[:, w, :], parts[:, w, 1, :], ALU.subtract).then_inc(s["part3"], 1)

            def scatter():
                pool.wait_ge(s["slots_zeroed"], 16 * E)
                pool.wait_ge(s["xn_kept"], B)
                for k in range(2):
                    pool.wait_ge(s["slots_ready"], k + 1)
                    for t in range(NT):
                        p.indirect_dma_start(scatter_rows, bass.IndirectOffsetOnAxis(ap=slot_out[:, k, t:t + 1], axis=0),
                                             xn_all[:, t * C:(t + 1) * C], None, bounds_check=E * CAP - 1,
                                             oob_is_err=False).then_inc(s[f"scattered{k}"], 16)

            def body(b, first, last):
                for j in range(QUADS):
                    g = QUADS * b + j
                    for u, unit in enumerate(UNITS):
                        n = NU * g + u
                        wait_first(pool, s["exp_done"], n + 1)
                        cols = probs[:, j % 2, u * 512:(u + 1) * 512]
                        if len(unit) == 1:
                            tile, pattern = cols[:, 0:P], [[1, P]]
                        else:
                            gap = unit[1][2]
                            tile, pattern = diagonal_blocks(cols, gap), [[0, 2], [1, P]]
                        p.affine_select(out=tile, in_=tile, compare_op=ALU.is_ge, fill=0.0, base=0, pattern=pattern,
                                        channel_multiplier=-1).then_inc(s["probs_masked"], 1)
                        if u == 3:
                            wait_first(pool, s["v_copied"], b + 1)
                            if not first:
                                wait_first(pool, s["pv_done"], QUADS * (b - 1) + j + 1)
                            p.tensor_scalar(vaug[:, j, :, :, 0:DK], vstage[:, :, 4 * j:4 * j + 4, :], 1.0, 0.0,
                                            ALU.mult, ALU.add).then_inc(s["vaug_ready"], 1)
                        if not last:
                            if j == 0 and u in (4, 6, 9):
                                split(b + 1, 0, (4, 6, 9).index(u))
                            if j == 0 and u == 8:
                                split(b + 1, 1, 0)
                            if j == 1 and u in (0, 2):
                                split(b + 1, 1, 1 + u // 2)

            def diagonal_blocks(cols, gap):
                if gap == 256:
                    return cols.rearrange("p (k n) -> p k n", k=2)[:, :, 0:P]
                return cols.rearrange("p (k n) -> p k n", k=4)[:, 0:4:3, :]

            for w in range(2):
                for k in range(3):
                    split(0, w, k)
            scatter()
            pool.wait_ge(s["init_done"], 5)
            body(0, True, False)
            body(1, False, False)
            with pool.Fori(2, B - 1) as b:
                body(b, False, False)
            body(B - 1, False, True)
            pool.wait_ge(s["eo_stored"], 16 * E)
            for t in range(NT):
                for k in range(2):
                    i = 2 * t + k
                    if i >= 4:
                        pool.wait_ge(s["combined"], i - 3)
                    p.indirect_dma_start(rows[:, i % 4, :], None, expert_rows,
                                         bass.IndirectOffsetOnAxis(ap=slot_in[:, k, t:t + 1], axis=0),
                                         bounds_check=E * CAP - 1, oob_is_err=False).then_inc(gathered[i % 4], 16)

        @block.scalar
        def _(act):
            a = nc.scalar
            act.wait_ge(s["biases_ready"], 1)
            a.copy(biases[:], bank_misc[:, 0:HJ * (E + 1)]).then_inc(s["biases_copied"], 1)
            act.wait_ge(s["biases_copied"], 1)
            def router(b):
                at_least(act, s["xnT_ready"], b + 1)
                a.copy(xnT[:, bass.ds(b * S, S)], bank_a[0][:]).then_inc(s["xnT_copied"], 1)
                for h in range(HJ):
                    at_least(act, s["hid_ready"], HJ * b + h + 1)
                    if h == 0:
                        at_least(act, s["lgT_ready"], b)
                    a.activation(hid[:, h, :], bank_o[h % 2][:], ACT.Relu, bias=biases[:, h:h + 1]).then_inc(s["hid_relu"], 1)
                at_least(act, s["lgT_ready"], b + 1)
                at_least(act, s["lg_ready"], b)
                a.copy(lgT[:], bank_b[0][:]).then_inc(s["lgT_copied"], 1)

            router(0)
            with act.Fori(1, B) as b:
                router(b)

            def part(b, w, k):
                i = 2 * b + w
                if k == 0:
                    act.wait_ge(s["rope_sum"], i + 1)
                    if not (isinstance(b, int) and b == 0):
                        act.wait_ge(s["qk_stored"], 96 * b)
                    a.copy(parts[:, w, 0, :], qk[:, w, :]).then_inc(s["part1"], 1)
                else:
                    act.wait_ge(s["rest1"], i + 1)
                    a.copy(parts[:, w, 1, :], qk[:, w, :]).then_inc(s["part2"], 1)

            def evict_o(b, j):
                g = QUADS * b + j
                act.wait_ge(s["pv_done"], g + 1)
                if not (isinstance(b, int) and g < 2):
                    act.wait_ge(o_stored[j % 2], 16 * (2 * b + j // 2))
                a.copy(osb[:, j % 2, :], bank_o[j % 2][:]).then_inc(s["o_copied"], 1)

            def body(b, first, last):
                for j in range(QUADS):
                    g = QUADS * b + j
                    for u in range(NU):
                        n = NU * g + u
                        act.wait_ge(s["scores_ready"], n + 1)
                        if u == 0 and not (first and j < 2):
                            act.wait_ge(s["pv_done"], g - 1)
                        a.activation(probs[:, j % 2, u * 512:(u + 1) * 512], bank_b[u % 2][:], ACT.Exp, scale=SCALE).then_inc(s["exp_done"], 1)
                        if j == 0 and u == 1:
                            act.wait_ge(s["v_ready"], b + 1)
                            if not first:
                                act.wait_ge(s["vaug_ready"], QUADS * b)
                            a.copy(vstage[:].rearrange("p t h d -> p (t h d)"), bank_misc[:]).then_inc(s["v_copied"], 1)
                        if not last:
                            if j == 0 and u in (5, 8):
                                part(b + 1, 0, (u - 5) // 3)
                            if j == 0 and u == 9:
                                part(b + 1, 1, 0)
                            if j == 1 and u == 2:
                                part(b + 1, 1, 1)
                        if u == 8:
                            if j > 0:
                                evict_o(b, j - 1)
                            elif not first:
                                evict_o(b - 1, 3)

            for w in range(2):
                for k in range(2):
                    part(0, w, k)
            act.wait_ge(s["gap_ready"], 1)
            a.activation(rs[4][:], rs[3][:], ACT.Exp).then_inc(s["gap_exp"], 1)
            act.wait_ge(s["scan_ready"], 2)
            a.copy(rt[2][:], bank_misc[:, 0:NT * E])
            a.copy(rt[3][:], bank_misc[:, NT * E:2 * NT * E]).then_inc(s["scan_copied"], 1)
            body(0, True, False)
            body(1, False, False)
            with act.Fori(2, B - 1) as b:
                body(b, False, False)
            body(B - 1, False, True)
            evict_o(B - 1, 3)
            def expert(e):
                at_least(act, s["dT_ready"], e + 1)
                at_least(act, s["eh_ready"], HJ * e)
                a.copy(dspT[:], bank_a[0][:]).then_inc(s["dT_copied"], 1)
                for h in range(HJ):
                    at_least(act, s["eh_ready"], HJ * e + h + 1)
                    if h == 0:
                        at_least(act, s["eo_ready"], e)
                    a.activation(hid[:, h, :], bank_b[h % 2][:], ACT.Relu, bias=biases[:, bass.ds(e * HJ + HJ + h, 1)]).then_inc(s["eh_relu"], 1)

            expert(0)
            with act.Fori(1, E) as e:
                expert(e)

        @block.tensor
        def _(pe):
            t = nc.tensor
            pe.wait_ge(s["consts_loaded"], 16 * len(CONSTS))
            pe.wait_ge(s["weights_loaded"], 144)
            pe.wait_ge(s["sums_init"], 2)
            t.transpose(bank_misc[:, 0:HJ * (E + 1)], bias_rows[:], ident[0:HJ * (E + 1), 0:HJ * (E + 1)]).then_inc(s["biases_ready"], 1)
            def router(b):
                at_least(pe, s["xn_ready"], b + 1)
                at_least(pe, s["xnT_copied"], b)
                for i in range(TS):
                    ins = t.transpose(bank_a[0][:, i * P:(i + 1) * P], xn[:, i, :], ident[:])
                ins.then_inc(s["xnT_ready"], 1)
                at_least(pe, s["xnT_copied"], b + 1)
                for h in range(HJ):
                    at_least(pe, s["hid_relu"], HJ * b + h - 1 if h else HJ * b)
                    t.matmul(bank_o[h % 2][:], w1r[:, h * P:(h + 1) * P], xnT[:, bass.ds(b * S, S)], start=True, stop=True).then_inc(s["hid_ready"], 1)
                at_least(pe, s["hid_relu"], HJ * b + HJ)
                at_least(pe, s["lgT_copied"], b)
                for h in range(HJ):
                    ins = t.matmul(bank_b[0][32 * h:32 * h + 32, :], w2r[:, h, :], hid[:, h, :], start=True, stop=True)
                ins.then_inc(s["lgT_ready"], 1)
                at_least(pe, s["lgT_copied"], b + 1)
                at_least(pe, s["logits_ready"], b)
                for i in range(TS):
                    ins = t.matmul(bank_b[1][:, i * E:(i + 1) * E], lgT[:, i * P:(i + 1) * P], sel[:], start=True, stop=True)
                ins.then_inc(s["lg_ready"], 1)

            router(0)
            with pe.Fori(1, B) as b:
                router(b)

            def project(b, w, k):
                i = 4 * b + 2 * w + k
                if not (isinstance(b, int) and i == 0):
                    pe.wait_ge(s["rope_mul"], i)
                t.matmul(bank_proj[:], ((wq, wqr), (wk, wkr))[w][k][:], xnT[:, bass.ds(b * S, S)], start=True, stop=True).then_inc(s["proj_ready"], 1)

            def project_v(b, first):
                pe.wait_ge(s["xv_loaded"], 16 * b + 16)
                if not first:
                    at_least(pe, s["res_added"], b - 1)
                    pe.wait_ge(s["negm_ready"], 2 * (QUADS * b + 1))
                else:
                    pe.wait_ge(s["negm_ready"], 2)
                for i in range(TS):
                    ins = t.matmul(bank_misc[:, i * P:(i + 1) * P], xv[:, i * P:(i + 1) * P], wv[:], start=True, stop=True)
                ins.then_inc(s["v_ready"], 1)

            def scores_a(b, j, n):
                h, qt = ATILES[n]
                g = QUADS * b + j
                if not (isinstance(b, int) and g == 0 and n < 2):
                    pe.wait_ge(s["rowmax_done"], NA * g + n - 1)
                if n == 0:
                    pe.wait_ge(slot_loaded[j], 48 * (b + 1))
                t.matmul(bank_a[n % 2][:, 0:P * (qt + 1)], Q[0:KROWS, j, h, qt * P:(qt + 1) * P], K[0:KROWS, j, h, 0:P * (qt + 1)],
                         start=True, stop=True).then_inc(s["a_ready"], 1)

            def turn_max(b, j):
                g = QUADS * b + j
                pe.wait_ge(s["rowmax_done"], NA * (g + 1))
                if not (isinstance(b, int) and g == 0):
                    pe.wait_ge(s["negm_ready"], 2 * g)
                    if j == 0:
                        pe.wait_ge(s["v_copied"], b)
                    else:
                        pe.wait_ge(s["v_copied"], b + 1)
                t.transpose(bank_misc[0:16, 0:P], rmax[:, j % 2, :], ident[:]).then_inc(s["mt_ready"], 1)

            def scores_b(b, j, u):
                n = NU * (QUADS * b + j) + u
                if not (isinstance(b, int) and n < 2):
                    pe.wait_ge(s["exp_done"], n - 1)
                if u == 0:
                    pe.wait_ge(m_loaded[j], 16 * (b + 1))
                for h, kt, c, w in UNITS[u]:
                    ins = t.matmul(bank_b[u % 2][:, c:c + w], K[0:KROWS, j, h, kt * P:(kt + 1) * P], Q[0:KROWS, j, h, kt * P:S],
                                   start=True, stop=True)
                ins.then_inc(s["scores_ready"], 1)

            def weigh_v(b, j, kt):
                g = QUADS * b + j
                if kt == 0:
                    pe.wait_ge(s["probs_masked"], NU * (g + 1))
                    pe.wait_ge(s["vaug_ready"], g + 1)
                    if not (isinstance(b, int) and g < 2):
                        pe.wait_ge(s["o_copied"], g - 1)
                for h in range(4):
                    at, w = PIECE[h, kt]
                    ins = t.matmul(bank_o[j % 2][VW * h:VW * h + VW, kt * P:S], vaug[:, j, kt, h, :], probs[:, j % 2, at:at + w],
                                   start=(kt == 0), stop=(kt == TS - 1), skip_group_check=True)
                if kt == TS - 1:
                    ins.then_inc(s["pv_done"], 1)

            def project_o(b, g_turned):
                pe.wait_ge(s["on_ready"], b + 1)
                pe.wait_ge(s["negm_ready"], 2 * g_turned)
                for i in range(TS):
                    ins = t.matmul(bank_misc[:, i * P:(i + 1) * P], oT[:, i * P:(i + 1) * P], wo[:], start=True, stop=True)
                ins.then_inc(s["out_ready"], 1)

            def body(b, first, last):
                for j in range(QUADS):
                    done = 0
                    for u in range(NU):
                        if j == 0 and u == 0:
                            project_v(b, first)
                        if j == 0 and not last and u in (1, 3, 5, 7):
                            project(b + 1, u // 4, (u // 2) % 2)
                        scores_b(b, j, u)
                        for _ in range(2 if u < 6 else 1):
                            if j < 2:
                                scores_a(b, j + 2, done)
                            elif not last:
                                scores_a(b + 1, j - 2, done)
                            done += 1
                        if u == 2:
                            if j < 3:
                                turn_max(b, j + 1)
                            elif not last:
                                turn_max(b + 1, 0)
                        if u in (1, 3, 5, 7):
                            if j > 0:
                                weigh_v(b, j - 1, u // 2)
                            elif not first:
                                weigh_v(b - 1, 3, u // 2)
                        if j == 3 and u == 8 and not first:
                            project_o(b - 1, QUADS * (b + 1) + (0 if last else 1))

            pe.wait_ge(s["rotated"], 4)
            for i in range(4):
                project(0, i // 2, i % 2)
            pe.wait_ge(s["biases_copied"], 1)
            pe.wait_ge(s["scan_ready"], 1)
            t.matmul(bank_misc[:, 0:NT * E], tri[:], rt[5][:], start=True, stop=True)
            t.matmul(bank_misc[:, NT * E:2 * NT * E], ones[:], rt[5][:], start=True, stop=True).then_inc(s["scan_ready"], 1)
            pe.wait_ge(s["logits_ready"], B)
            pe.wait_ge(s["scan_copied"], 1)
            for j in range(2):
                for n in range(NA):
                    scores_a(0, j, n)
                if j == 0:
                    turn_max(0, 0)
            body(0, True, False)
            body(1, False, False)
            with pe.Fori(2, B - 1) as b:
                body(b, False, False)
            body(B - 1, False, True)
            for kt in range(TS):
                weigh_v(B - 1, 3, kt)
            pe.wait_ge(s["res_added"], B - 1)
            project_o(B - 1, QUADS * B)

            def expert(e):
                at_least(pe, s["disp_loaded"], 16 * e + 16)
                at_least(pe, s["dT_copied"], e)
                for i in range(TS):
                    ins = t.transpose(bank_a[0][:, i * P:(i + 1) * P], dsp[:, i, :], ident[:])
                ins.then_inc(s["dT_ready"], 1)
                at_least(pe, s["dT_copied"], e + 1)
                at_least(pe, s["ew_loaded"], 48 * e + 48)
                for h in range(HJ):
                    at_least(pe, s["eh_relu"], HJ * e + h - 1 if h else HJ * e)
                    t.matmul(bank_b[h % 2][:], w1s[:, h * P:(h + 1) * P], dspT[:], start=True, stop=True).then_inc(s["eh_ready"], 1)
                at_least(pe, s["eh_relu"], HJ * e + HJ)
                at_least(pe, s["eo_copied"], e)
                for i in range(TS):
                    for h in range(HJ):
                        ins = t.matmul(bank_o[0][:, i * P:(i + 1) * P], hid[:, h, i * P:(i + 1) * P], w2s[:, h, :],
                                       start=(h == 0), stop=(h == HJ - 1))
                ins.then_inc(s["eo_ready"], 1)

            expert(0)
            with pe.Fori(1, E) as e:
                expert(e)


def constants(S, DK, E, CAP):
    import numpy as np
    f = np.float32
    pos = np.arange(S, dtype=f)
    inv = (f(1.0) / np.power(f(10000.0), np.arange(0, DK, 2, dtype=f) / f(DK))).astype(f)
    angles = np.outer(pos, inv).astype(f)
    cos = np.repeat(np.cos(angles), 2, axis=-1).astype(f)
    sin = np.repeat(np.sin(angles), 2, axis=-1).astype(f)
    q = np.arange(P)
    amask = np.zeros((P, S), f)
    amask[:, S - P:] = np.where(q[None, :] <= q[:, None], 0.0, -BIG)
    sel = np.zeros((P, E), f)
    for h in range(4):
        sel[32 * h + np.arange(E), np.arange(E)] = 1.0
    erow = np.concatenate([E - np.arange(E), CAP * np.arange(E)]).astype(f)
    return {
        "ident": np.eye(P, dtype=f),
        "cosT": np.ascontiguousarray(np.tile(cos.T, (HEADS, 1))),
        "sinT": np.ascontiguousarray(np.tile(sin.T, (HEADS, 1))),
        "amask": amask,
        "tri": (q[:, None] <= q[None, :]).astype(f),
        "sel": sel,
        "erow": np.ascontiguousarray(np.tile(erow, (P, 1))),
        "zeros": np.zeros((2, 2 * S), f),
    }


_INS = ["L0_attn_x", "L0_attn_Wq", "L0_attn_Wk", "L0_attn_Wv", "L0_attn_Wo", "L0_ffn_rw1", "L0_ffn_rb1",
        "L0_ffn_rw2", "L0_ffn_rb2", "L0_ffn_ew1", "L0_ffn_eb1", "L0_ffn_ew2", "L0_ffn_eb2"]


def kernel(**inputs):
    import numpy as _np
    import concourse.bacc as _bacc
    from concourse import mybir as _mybir
    from concourse.bass_utils import run_bass_kernel_spmd as _run

    nc = _bacc.Bacc("TRN2", target_bir_lowering=False, num_devices=1)
    B, S, C = inputs["L0_attn_x"].shape
    E = inputs["L0_ffn_ew1"].shape[0]
    arrays, args = {}, []
    named = {n: _np.ascontiguousarray(inputs[n]) for n in _INS}
    named.update(constants(S, C // HEADS, E, S))
    for name, a in named.items():
        arrays[f"in_{name}_dram"] = a
        args.append(nc.dram_tensor(f"in_{name}_dram", a.shape, _mybir.dt.from_np(a.dtype), kind="ExternalInput").ap())
    args.append(nc.dram_tensor("out_0_dram", (B, S, C), F32, kind="ExternalOutput").ap())
    build(nc, *args)
    r = _run(nc, [arrays], core_ids=[0])
    return r.results[0]["out_0_dram"]
```

```python
from contextlib import ExitStack

import concourse.bass as bass
from concourse import mybir

F32 = mybir.dt.float32
BF16 = mybir.dt.bfloat16
U32 = mybir.dt.uint32
ALU = mybir.AluOpType
ACT = mybir.ActivationFunctionType
AXX = mybir.AxisListType.X

P = 128
HEADS = 16
PARTS = 3
TERMS = PARTS * PARTS
EPS = 1e-5
BIG = 3.0e38
FAR_SLOT = 65536.0
ROW = 132
TOKEN, FIRST, GAP, SECOND = 128, 129, 130, 131
EXPERT_FROM = 3


def at_least(eng, sem, value):
    if not isinstance(value, int) or value > 0:
        eng.wait_ge(sem, value)


def wait_first(eng, passed, sem, value):
    at_least(eng, sem, value)
    if not isinstance(value, int):
        eng.sem_inc(passed, 1)


def build(nc, x, Wq, Wk, Wv, Wo, rw1, rb1, rw2, rb2, ew1, eb1, ew2, eb2,
          ident_in, cos_in, sin_in, amask_in, tri_in, sel_in, erow_in, token_in, trash_in, zeros_in, out):
    B, S, C = x.shape
    E, _, H = ew1.shape
    CAP = S
    N = B * S
    NT = N // P
    TS = S // P
    HJ = H // P
    DK = C // HEADS
    QUADS = HEADS // 4
    MROW = TERMS * DK
    KROWS = 96
    SCALE = float(DK) ** -0.5
    VW = 32
    TOPS = 13
    assert (C, S, TS, QUADS, HJ) == (P, 512, 4, 4, 4) and 2 * (B - 1 - EXPERT_FROM) == E

    PAIR_UNITS = [[(0, 0, 0, 512)], [(0, 1, 0, 384), (0, 3, 384, 128)],
                  [(1, 0, 0, 512)], [(1, 1, 0, 384), (1, 3, 384, 128)],
                  [(0, 2, 0, 256), (1, 2, 256, 256)]]
    UNITS = [[(2 * i + h, kt, c, n) for h, kt, c, n in unit] for i in range(2) for unit in PAIR_UNITS]
    NU = len(UNITS)
    PIECE = {(h, kt): (u * 512 + c, n) for u, unit in enumerate(UNITS) for h, kt, c, n in unit}
    AUNITS = [(h, tiles) for h in range(4) for tiles in ([(0, 0), (1, P)], [(2, 0)], [(3, 0)])]
    NA = len(AUNITS)
    A_BESIDE = [2, 1, 1, 1, 1, 2, 1, 1, 1, 1]
    SCATTERS = [(k, t) for k in range(2) for t in range(NT)]
    SPREAD = EXPERT_FROM * QUADS * NU

    slot_rows = nc.dram_tensor("slot_rows", (E * CAP, ROW), F32, kind="Internal").ap()
    ffn_rows = nc.dram_tensor("ffn_rows", (N + CAP, C), F32, kind="Internal").ap()
    qk_dram = nc.dram_tensor("qk_dram", (B * 2 * P, TERMS * S), BF16, kind="Internal").ap()
    m_dram = nc.dram_tensor("m_dram", (B * QUADS * 16, 2 * P), BF16, kind="Internal").ap()
    o_dram = nc.dram_tensor("o_dram", (B * QUADS * P, S), F32, kind="Internal").ap()
    oc_dram = nc.dram_tensor("oc_dram", (B * P, S), F32, kind="Internal").ap()
    d_dram = nc.dram_tensor("d_dram", (B * HEADS, S), F32, kind="Internal").ap()
    rb_dram = nc.dram_tensor("rb_dram", (B * P, S), F32, kind="Internal").ap()
    r_dram = nc.dram_tensor("r_dram", (B * HEADS, S), F32, kind="Internal").ap()

    with ExitStack() as ctx:
        def sb(name, shape, dt=F32):
            return ctx.enter_context(nc.sbuf_tensor(name, shape, dt))

        def sem(name):
            return ctx.enter_context(nc.semaphore(name))

        banks = [ctx.enter_context(nc.psum_tensor(f"bank{i}", [P, 512], F32)) for i in range(8)]
        bank_a = banks[0:3]
        bank_b = banks[3:5]
        bank_o = banks[5]
        bank_proj = banks[6]
        bank_misc = banks[7]

        ident = sb("ident", [P, P])
        cosT = sb("cosT", [P, S])
        sinT = sb("sinT", [P, S])
        amask = sb("amask", [P, S])
        tri = sb("tri", [P, P])
        ones = sb("ones", [P, P])
        sel = sb("sel", [P, E])
        erow = sb("erow", [P, 2 * E])
        trash = sb("trash", [P, TS])
        wq = sb("wq", [P, C])
        wk = sb("wk", [P, C])
        wqr = sb("wqr", [P, C])
        wkr = sb("wkr", [P, C])
        wv = sb("wv", [P, C])
        wo = sb("wo", [P, C])
        bias_rows = sb("bias_rows", [HJ * (E + 1), P])
        biases = sb("biases", [P, HJ * (E + 1)])
        w2r = sb("w2r", [P, HJ, 32])
        b2r = sb("b2r", [P, E])
        res = sb("res", [P, NT * C])
        xrow = sb("xrow", [P, NT, ROW])
        xnT = sb("xnT", [P, N])
        xn = sb("xn", [P, TS, C])
        stats = sb("stats", [P, TS, 6])
        mv = sb("mv", [P, TS, 2])
        vpe = sb("vpe", [P, TS])
        nhalf = sb("nhalf", [P, TS])
        rstd = sb("rstd", [P, TS])
        hid = sb("hid", [P, HJ, S])
        lgT = sb("lgT", [P, S])
        dspT = lgT
        lg = [sb(f"lg{i}", [P, TS * E]) for i in range(4)]
        top = [sb(f"top{i}", [P, TS]) for i in range(3)]
        hot = [sb(f"hot{k}", [P, NT * E]) for k in range(2)]
        picked = sb("picked", [P, NT * E])
        within = sb("within", [P, NT * E])
        totals = sb("totals", [P, NT * E])
        before = sb("before", [P, NT * E])
        gap = sb("gap", [P, NT])
        small = [sb(f"small{i}", [P, NT]) for i in range(8)]
        slot = sb("slot", [P, 2, NT], U32)
        w1s = sb("w1s", [P, 2, H])
        w1r = w1s[:, 0]
        w2s = sb("w2s", [P, 2, HJ, C])
        b2s = sb("b2s", [P, 2, C])
        dsp = sb("dsp", [P, TS, ROW])
        ew = [sb(f"ew{i}", [P, TS]) for i in range(5)]
        back = sb("back", [P, TS], U32)
        eo = sb("eo", [P, TS * C])
        xv = sb("xv", [P, S])
        rope = sb("rope", [P, 4, S])
        qk = sb("qk", [P, 2, S])
        parts = sb("parts", [P, 2, PARTS, S], BF16)
        Q = sb("Q", [P, QUADS, 4, S], BF16)
        K = sb("K", [P, QUADS, 4, S], BF16)
        rmax = sb("rmax", [P, 2, 16])
        negm = sb("negm", [16, 2, P], BF16)
        probs = sb("probs", [P, 2, NU * 512])
        vstage = sb("vstage", [P, TS, HEADS, DK])
        vaug = sb("vaug", [P, QUADS, TS, 4, VW])
        osb = sb("osb", [P, 2, S])
        oT = sb("oT", [P, S])
        dcomp = sb("dcomp", [P, 64])
        rcomp = sb("rcomp", [P, 64])
        rbc = sb("rbc", [P, S])
        zrow = sb("zrow", [P, TS * ROW])
        ffn = rope

        s = {}
        for name in """ident_loaded bias_loaded router_loaded route_loaded attn_loaded x_loaded w2r_zero zrow_zero
            sums_init init_done rotated
            var_ready rstd_ready xn_ready xn_kept xnT_ready xnT_copied hid_ready hid_relu lgT_ready lgT_copied
            lg_ready topped biases_ready biases_copied picked_ready counts_ready counts_copied gap_exp
            route slots_ready rows_ready slots_zeroed ffn_zeroed scattered
            xv_loaded v_ready v_copied vaug_ready proj_ready rope_mul rope_sum part1 rest1 part2 part3
            qk_stored a_ready rowmax_done mt_ready negm_ready m_stored scores_ready exp_done probs_masked
            pv_done o_copied d_closed o_closed d_loaded o_loaded rec_ready rec_stored rec_spread rbc_loaded
            on_ready out_ready res_added
            dT_ready dT_copied weighed eh_ready eh_relu eo_ready eo_biased eo_ready_out eo_added weighing
            ffn_added out_stored dve_passed pool_passed""".split():
            s[name] = sem(name)
        slot_loaded = [sem(f"slot_loaded{j}") for j in range(QUADS)]
        m_loaded = [sem(f"m_loaded{j}") for j in range(QUADS)]
        o_stored = [sem(f"o_stored{p}") for p in range(2)]
        ew_loaded = [sem(f"ew_loaded{i}") for i in range(2)]
        ffn_loaded = [sem(f"ffn_loaded{i}") for i in range(2)]

        block = ctx.enter_context(nc.Block())

        def begun(b):
            return not (isinstance(b, int) and b == 0)

        def sequences(body, eng):
            for b in range(EXPERT_FROM + 1):
                body(b, b >= EXPERT_FROM)
            with eng.Fori(EXPERT_FROM + 1, B - 1) as b:
                body(b, True)
            body(B - 1, False)

        def router_steps(body, eng):
            body(0)
            body(1)
            with eng.Fori(2, B - 1) as b:
                body(b)
            body(B - 1)

        def is_last(b):
            return isinstance(b, int) and b == B - 1

        @block.sync
        def _(sp):
            xt = x.rearrange("b (t p) c -> p (b t) c", p=P)
            ot = out.rearrange("b (t p) c -> p (b t) c", p=P)
            rest = res[:].rearrange("p (t c) -> p t c", c=C)

            def load_x(b):
                at_least(sp, s["x_loaded"], 16 * b)
                sp.dma_start(rest[:, bass.ds(b * TS, TS), :], xt[:, bass.ds(b * TS, TS), :]).then_inc(s["x_loaded"], 16)

            load_x(0)
            with sp.Fori(1, B) as b:
                load_x(b)

            def store_parts(b, w):
                sp.wait_ge(s["part3"], 2 * b + w + 1)
                dst = qk_dram[bass.ds((2 * b + w) * P, P), :].rearrange("p (i j n) -> p i j n", i=PARTS, j=PARTS)
                for r in range(PARTS):
                    sp.dma_start(dst[:, :, r, :] if w == 0 else dst[:, r, :, :], parts[:, w]).then_inc(s["qk_stored"], 16)

            def load_slot(b, j):
                sp.wait_ge(s["qk_stored"], 96 * b + 96)
                for w, dst in ((0, Q), (1, K)):
                    src = qk_dram[bass.ds((2 * b + w) * P + j * 4 * DK, 4 * DK), :].rearrange("(h d) (t n) -> (d t) h n", d=DK, t=TERMS)
                    sp.dma_start(dst[0:MROW, j], src).then_inc(slot_loaded[j], 16)
                sp.dma_start(Q[MROW:MROW + 2, j].rearrange("p h n -> p (h n)").bitcast(F32), zeros_in).then_inc(slot_loaded[j], 16)

            def next_slot(b, j):
                sp.wait_ge(s["scores_ready"], NU * (QUADS * b + j + 1))
                load_slot(b + 1, j)

            def load_max(b, j):
                g = QUADS * b + j
                sp.wait_ge(s["negm_ready"], 2 * g + 2)
                md = m_dram[bass.ds(g * 16, 16), :]
                sp.dma_start(md, negm[:].rearrange("p k q -> p (k q)")).then_inc(s["m_stored"], 16)
                sp.wait_ge(s["m_stored"], 16 * g + 16)
                sp.wait_ge(s["rowmax_done"], 16 * (g + 1))
                sp.dma_start(Q[MROW:MROW + 2, j].rearrange("p h (t q) -> p (h t) q", q=P),
                             md.rearrange("a (k q) -> k a q", k=2)).then_inc(m_loaded[j], 16)

            def store_o(b, j):
                g = QUADS * b + j
                sp.wait_ge(s["o_copied"], g + 1)
                sp.dma_start(o_dram[bass.ds(g * P, P), :], osb[:, j % 2, :]).then_inc(o_stored[j % 2], 16)

            def finish_gather(b):
                for p in range(2):
                    sp.wait_ge(o_stored[p], 16 * (2 * b + 2))
                od = o_dram[bass.ds(b * QUADS * P, QUADS * P), :].rearrange("(h r) n -> h r n", r=VW)
                sp.dma_start(d_dram[bass.ds(b * HEADS, HEADS), :], od[:, DK, :]).then_inc(s["d_closed"], 16)
                sp.dma_start(oc_dram[bass.ds(b * P, P), :].rearrange("(h d) n -> h d n", d=DK), od[:, 0:DK, :]).then_inc(s["o_closed"], 16)

            def finish_loads(b):
                sp.wait_ge(s["d_closed"], 16 * b + 16)
                sp.dma_start(dcomp[:], d_dram[bass.ds(b * HEADS, HEADS), :].rearrange("h (a n) -> (h a) n", n=64)).then_inc(s["d_loaded"], 16)
                sp.wait_ge(s["o_closed"], 16 * b + 16)
                at_least(sp, s["out_ready"], b)
                sp.dma_start(oT[:], oc_dram[bass.ds(b * P, P), :]).then_inc(s["o_loaded"], 16)

            def store_recip(b):
                sp.wait_ge(s["rec_ready"], b + 1)
                sp.dma_start(r_dram[bass.ds(b * HEADS, HEADS), :].rearrange("h (a n) -> (h a) n", n=64), rcomp[:]).then_inc(s["rec_stored"], 16)

            def spread_recip(b):
                sp.wait_ge(s["rec_stored"], 16 * b + 16)
                src = r_dram[bass.ds(b * HEADS, HEADS), :].rearrange("h (o n) -> h o n", o=1).broadcast_to([HEADS, DK, S])
                sp.dma_start(rb_dram[bass.ds(b * P, P), :].rearrange("(h d) n -> h d n", d=DK), src).then_inc(s["rec_spread"], 16)

            def load_recip(b):
                sp.wait_ge(s["rec_spread"], 16 * b + 16)
                at_least(sp, s["on_ready"], b)
                sp.dma_start(rbc[:], rb_dram[bass.ds(b * P, P), :]).then_inc(s["rbc_loaded"], 16)

            def load_xv(b):
                at_least(sp, s["v_ready"], b)
                sp.dma_start(xv[:], xnT[:, bass.ds(b * S, S)]).then_inc(s["xv_loaded"], 16)

            def load_expert(e, i):
                if i == 0:
                    sp.wait_ge(s["scattered"], 16 * 2 * NT)
                if i == 0:
                    at_least(sp, s["eo_biased"], e - 1)
                at_least(sp, s["dT_ready"], e)
                at_least(sp, s["weighed"], e)
                if i == 1:
                    at_least(sp, s["eo_biased"], e - 1)
                sp.dma_start(dsp[:], slot_rows[bass.ds(e * CAP, CAP), :].rearrange("(t p) c -> p t c", p=P)).then_inc(ew_loaded[i], 16)
                sp.dma_start(w1s[:, i], ew1.rearrange("e c h -> (e c) h")[bass.ds(e * C, C), :]).then_inc(ew_loaded[i], 16)
                sp.dma_start(w2s[:, i], ew2.rearrange("e h c -> (e h) c")[bass.ds(e * H, H), :].rearrange("(j p) c -> p j c", p=P)).then_inc(ew_loaded[i], 16)
                sp.dma_start(b2s[:, i], eb2[bass.ds(e, 1), :].broadcast_to([P, C])).then_inc(ew_loaded[i], 16)

            def body(b, experts):
                last = is_last(b)
                e = 2 * (b - EXPERT_FROM)
                load_xv(b)
                if begun(b):
                    next_slot(b - 1, 3)
                else:
                    load_slot(b, 3)
                if experts:
                    load_expert(e, 0)
                load_max(b, 1)
                if begun(b):
                    store_o(b - 1, 3)
                if not last:
                    store_parts(b + 1, 0)
                if begun(b):
                    finish_gather(b - 1)
                if not last:
                    store_parts(b + 1, 1)
                    next_slot(b, 0)
                load_max(b, 2)
                if begun(b):
                    finish_loads(b - 1)
                store_o(b, 0)
                if experts:
                    load_expert(e + 1, 1)
                if not last:
                    next_slot(b, 1)
                load_max(b, 3)
                if begun(b):
                    store_recip(b - 1)
                store_o(b, 1)
                if begun(b):
                    spread_recip(b - 1)
                if not last:
                    next_slot(b, 2)
                if begun(b):
                    load_recip(b - 1)
                if not last:
                    load_max(b + 1, 0)
                store_o(b, 2)

            def load_ffn(b):
                at_least(sp, s["ffn_added"], b - 1)
                sp.dma_start(ffn[:, b % 2, :].rearrange("p (t c) -> p t c", c=C),
                             ffn_rows[b * S:(b + 1) * S, :].rearrange("(t p) c -> p t c", p=P)).then_inc(ffn_loaded[b % 2], 16)

            def store_out(b):
                sp.wait_ge(s["ffn_added"], b + 1)
                sp.dma_start(ot[:, b * TS:(b + 1) * TS, :], rest[:, b * TS:(b + 1) * TS, :]).then_inc(s["out_stored"], 16)

            sp.wait_ge(s["init_done"], 4)
            store_parts(0, 0)
            store_parts(0, 1)
            for j in range(3):
                load_slot(0, j)
            load_max(0, 0)
            sequences(body, sp)
            store_o(B - 1, 3)
            finish_gather(B - 1)
            finish_loads(B - 1)
            sp.wait_ge(s["eo_added"], 16 * TS * E)
            sp.wait_ge(s["rope_sum"], 2 * B)
            load_ffn(0)
            load_ffn(1)
            store_recip(B - 1)
            spread_recip(B - 1)
            load_recip(B - 1)
            for b in range(B):
                if b + 2 < B:
                    load_ffn(b + 2)
                store_out(b)
            sp.wait_ge(s["out_stored"], 16 * B)

        @block.vector
        def _(dve):
            v = nc.vector
            v.memset(w2r[:], 0.0).then_inc(s["w2r_zero"], 1)
            v.memset(zrow[:], 0.0).then_inc(s["zrow_zero"], 1)
            v.memset(nhalf[:], -0.5).then_inc(s["sums_init"], 1)

            def layer_norm(b):
                dve.wait_ge(s["x_loaded"], 16 * b + 16)
                xs = res[:, bass.ds(b * TS * C, TS * C)].rearrange("p (t c) -> p t c", c=C)
                for t in range(TS):
                    ins = v.bn_stats(stats[:, t, :], xs[:, t, :])
                ins.then_inc(s["var_ready"], 1)
                wait_first(dve, s["dve_passed"], s["var_ready"], 3 * b + 1)
                for t in range(TS):
                    ins = v.bn_aggr(mv[:, t, :], stats[:, t, :])
                ins.then_inc(s["var_ready"], 1)
                dve.wait_ge(s["var_ready"], 3 * b + 2)
                v.tensor_scalar(vpe[:], mv[:, :, 1], EPS, None, ALU.add).then_inc(s["var_ready"], 1)
                dve.wait_ge(s["rstd_ready"], b + 1)
                at_least(dve, s["xnT_ready"], b)
                at_least(dve, s["xn_kept"], b)
                for t in range(TS):
                    ins = v.tensor_scalar(xn[:, t, :], xs[:, t, :], mv[:, t, 0:1], rstd[:, t:t + 1], ALU.subtract, ALU.mult)
                ins.then_inc(s["xn_ready"], 1)

            def grid(a):
                return a.rearrange("p (t e) -> p t e", e=E)

            def wide(a, tiles):
                return a.rearrange("p (t o) -> p t o", o=1).broadcast_to([P, tiles, E])

            def per_expert(a, tiles):
                return a.rearrange("p (o e) -> p o e", o=1).broadcast_to([P, tiles, E])

            def top_two(b):
                n = TOPS * b

                def next_step(ins, k):
                    ins.then_inc(s["topped"], 1)
                    dve.wait_ge(s["topped"], n + k)

                cols = bass.ds(b * TS * E, TS * E)
                pref = per_expert(erow[:, 0:E], TS)
                dve.wait_ge(s["lg_ready"], b + 1)
                next_step(v.tensor_tensor(grid(lg[0][:]), grid(bank_proj[:, 0:TS * E]), per_expert(b2r[:], TS), ALU.add), 1)
                for k in range(2):
                    cur, i = (lg[0], 1) if k == 0 else (lg[3], 7)
                    next_step(v.tensor_reduce(top[k][:], grid(cur[:]), AXX, ALU.max), i + 1)
                    next_step(v.tensor_tensor(grid(lg[1][:]), grid(cur[:]), wide(top[k][:], TS), ALU.is_equal), i + 2)
                    next_step(v.tensor_tensor(grid(lg[2][:]), grid(lg[1][:]), pref, ALU.mult), i + 3)
                    next_step(v.tensor_reduce(top[2][:], grid(lg[2][:]), AXX, ALU.max), i + 4)
                    next_step(v.tensor_tensor(grid(hot[k][:, cols]), grid(lg[2][:]), wide(top[2][:], TS), ALU.is_equal), i + 5)
                    if k == 0:
                        next_step(v.scalar_tensor_tensor(out=lg[3][:], in0=hot[0][:, cols], scalar=-BIG, in1=lg[0][:],
                                                         op0=ALU.mult, op1=ALU.add), 7)
                next_step(v.tensor_tensor(gap[:, bass.ds(b * TS, TS)], top[1][:], top[0][:], ALU.subtract), TOPS)

            def router(b):
                if not is_last(b):
                    layer_norm(b + 1)
                if begun(b):
                    top_two(b - 1)

            layer_norm(0)
            v.memset(ones[:], 1.0).then_inc(s["sums_init"], 1)
            v.memset(Q[64:KROWS], 0.0).then_inc(s["init_done"], 1)
            v.memset(K[64:KROWS], 1.0).then_inc(s["init_done"], 1)
            v.memset(vaug[:, 0:2], 1.0).then_inc(s["init_done"], 1)
            v.memset(vaug[:, 2:4], 1.0).then_inc(s["init_done"], 1)
            dve.wait_ge(s["attn_loaded"], 16 * 7)
            for w, wr in ((wq, wqr), (wk, wkr)):
                src = w[:].rearrange("p (i k) -> p i k", k=2)
                dst = wr[:].rearrange("p (i k) -> p i k", k=2)
                v.tensor_scalar(dst[:, :, 0], src[:, :, 1], -1.0, None, ALU.mult).then_inc(s["rotated"], 1)
                v.tensor_copy(dst[:, :, 1], src[:, :, 0]).then_inc(s["rotated"], 1)
            dve.wait_ge(s["route_loaded"], 16 * 4)
            dve.wait_ge(s["router_loaded"], 16 * 4)
            router_steps(router, dve)

            def ropes(b, w, k):
                dve.wait_ge(s["proj_ready"], 4 * b + 2 * w + k + 1)
                at_least(dve, s["rope_sum"], 2 * (b - 1) + w + 1)
                v.tensor_tensor(rope[:, 2 * w + k, :], bank_proj[:], (cosT if k == 0 else sinT)[:], ALU.mult).then_inc(s["rope_mul"], 1)

            def split(b, w, k):
                i = 2 * b + w
                if k == 0:
                    dve.wait_ge(s["rope_mul"], 2 * i + 2)
                    at_least(dve, s["part3"], i - 1)
                    v.tensor_tensor(qk[:, w, :], rope[:, 2 * w, :], rope[:, 2 * w + 1, :], ALU.add).then_inc(s["rope_sum"], 1)
                elif k == 1:
                    dve.wait_ge(s["part1"], i + 1)
                    v.tensor_tensor(qk[:, w, :], qk[:, w, :], parts[:, w, 0, :], ALU.subtract).then_inc(s["rest1"], 1)
                else:
                    dve.wait_ge(s["part2"], i + 1)
                    v.tensor_tensor(parts[:, w, 2, :], qk[:, w, :], parts[:, w, 1, :], ALU.subtract).then_inc(s["part3"], 1)

            def rowmax(b, j, a):
                h, tiles = AUNITS[a]
                g = QUADS * b + j
                bank = bank_a[a % 3]
                if a == 0:
                    at_least(dve, s["mt_ready"], g - 1)
                wait_first(dve, s["dve_passed"], s["a_ready"], NA * g + a + 1)
                for qt, c in tiles:
                    n = P * (qt + 1)
                    v.tensor_tensor_reduce(bank[:, c:c + n], bank[:, c:c + n], amask[:, S - n:S], 1.0, -BIG, ALU.add, ALU.max,
                                           rmax[:, j % 2, 4 * h + qt:4 * h + qt + 1]).then_inc(s["rowmax_done"], 1)

            def neg_max(b, j):
                g = QUADS * b + j
                dve.wait_ge(s["mt_ready"], g + 1)
                at_least(dve, s["m_stored"], 16 * g)
                v.tensor_scalar(negm[:, 0, :], bank_misc[0:16, 0:P], -1.0, None, ALU.mult).then_inc(s["negm_ready"], 1)
                dve.wait_ge(s["negm_ready"], 2 * g + 1)
                v.scalar_tensor_tensor(out=negm[:, 1, :], in0=bank_misc[0:16, 0:P], scalar=-1.0, in1=negm[:, 0, :],
                                       op0=ALU.mult, op1=ALU.subtract).then_inc(s["negm_ready"], 1)

            def finish_recip(b):
                dve.wait_ge(s["d_loaded"], 16 * b + 16)
                at_least(dve, s["rec_stored"], 16 * b)
                v.reciprocal(rcomp[:], dcomp[:]).then_inc(s["rec_ready"], 1)

            def finish_norm(b):
                dve.wait_ge(s["o_loaded"], 16 * b + 16)
                dve.wait_ge(s["rbc_loaded"], 16 * b + 16)
                v.tensor_tensor(oT[:], oT[:], rbc[:], ALU.mult).then_inc(s["on_ready"], 1)

            def finish_add(b):
                dve.wait_ge(s["out_ready"], b + 1)
                r = res[:, bass.ds(b * S, S)]
                v.tensor_tensor(r, bank_misc[:], r, ALU.add).then_inc(s["res_added"], 1)

            def weigh(e, i):
                dve.wait_ge(ew_loaded[i], 32 * (e - i) + 64)
                n = 6 * e

                def next_step(ins, k):
                    ins.then_inc(s["weighing"], 1)
                    dve.wait_ge(s["weighing"], n + k)

                first = erow[:, bass.ds(E + e, 1)]
                next_step(v.tensor_scalar(ew[0][:], dsp[:, :, FIRST], first, None, ALU.is_equal), 1)
                next_step(v.tensor_tensor(ew[1][:], ew[0][:], dsp[:, :, GAP], ALU.mult), 2)
                next_step(v.tensor_scalar(ew[2][:], dsp[:, :, TOKEN], 0.0, None, ALU.is_equal), 3)
                next_step(v.tensor_tensor(ew[4][:], ew[2][:], trash[:], ALU.mult), 4)
                at_least(dve, s["eo_added"], 16 * TS * e)
                next_step(v.tensor_tensor(ew[3][:], ew[1][:], dsp[:, :, SECOND], ALU.add), 5)
                next_step(v.scalar_tensor_tensor(out=back[:], in0=dsp[:, :, TOKEN], scalar=-1.0, in1=ew[4][:],
                                                 op0=ALU.add, op1=ALU.add), 6)
                v.tensor_copy(ew[0][:, 0:1], ew[3][:, 0:1]).then_inc(s["weighed"], 1)

            def expert_out(e, i):
                tc = "p (t c) -> p t c"
                dve.wait_ge(s["eo_ready"], e + 1)
                at_least(dve, s["eo_added"], 16 * TS * e)
                v.tensor_tensor(eo[:].rearrange(tc, c=C), bank_proj[:].rearrange(tc, c=C),
                                b2s[:, i].rearrange("p (o c) -> p o c", o=1).broadcast_to([P, TS, C]), ALU.add).then_inc(s["eo_biased"], 1)
                dve.wait_ge(s["eo_biased"], e + 1)
                v.tensor_tensor(eo[:].rearrange(tc, c=C), eo[:].rearrange(tc, c=C),
                                ew[3][:].rearrange("p (t o) -> p t o", o=1).broadcast_to([P, TS, C]), ALU.mult).then_inc(s["eo_ready_out"], 1)

            def body(b, experts):
                last = is_last(b)
                e = 2 * (b - EXPERT_FROM)
                for j in range(QUADS):
                    for a in range(NA):
                        if j < 2:
                            rowmax(b, j + 2, a)
                        elif not last:
                            rowmax(b + 1, j - 2, a)
                        if a == 4 and j < 3:
                            neg_max(b, j + 1)
                        elif a == 4 and not last:
                            neg_max(b + 1, 0)
                        if j == 0 and not last:
                            if a in (1, 3, 6, 8):
                                i = (1, 3, 6, 8).index(a)
                                ropes(b + 1, i // 2, i % 2)
                            if a == 4:
                                split(b + 1, 0, 0)
                            if a == 7:
                                split(b + 1, 0, 1)
                            if a == 9:
                                split(b + 1, 1, 0)
                            if a == 10:
                                split(b + 1, 0, 2)
                            if a == 11:
                                split(b + 1, 1, 1)
                        if j == 1 and a == 1 and not last:
                            split(b + 1, 1, 2)
                        if begun(b):
                            if (j, a) == (2, 1):
                                finish_recip(b - 1)
                            if (j, a) == (3, 7):
                                finish_norm(b - 1)
                            if (j, a) == (3, 11):
                                finish_add(b - 1)
                        if experts:
                            if (j, a) == (1, 2):
                                weigh(e, 0)
                            if (j, a) == (2, 2):
                                expert_out(e, 0)
                            if (j, a) == (2, 7):
                                weigh(e + 1, 1)
                            if (j, a) == (3, 2):
                                expert_out(e + 1, 1)

            top_two(B - 1)
            for w in range(2):
                for k in range(2):
                    ropes(0, w, k)
                for k in range(3):
                    split(0, w, k)

            count = [0]

            def step(ins):
                count[0] += 1
                ins.then_inc(s["route"], 1)
                dve.wait_ge(s["route"], count[0])

            base = per_expert(erow[:, E:2 * E], NT)
            v.tensor_tensor(picked[:], hot[0][:], hot[1][:], ALU.add).then_inc(s["picked_ready"], 1)
            dve.wait_ge(s["gap_exp"], 1)
            step(v.tensor_scalar(small[1][:], small[0][:], 1.0, None, ALU.add))
            step(v.reciprocal(small[2][:], small[1][:]))
            step(v.tensor_tensor(xrow[:, :, SECOND], small[0][:], small[2][:], ALU.mult))
            step(v.tensor_tensor(xrow[:, :, GAP], small[2][:], xrow[:, :, SECOND], ALU.subtract))
            dve.wait_ge(s["counts_copied"], 1)
            for e in range(E):
                ins = v.tensor_tensor_scan(grid(before[:])[:, :, e], grid(totals[:])[:, :, e], zrow[:, 0:NT], 0.0, ALU.add, ALU.add)
            step(ins)
            step(v.tensor_tensor(before[:], before[:], totals[:], ALU.subtract))
            step(v.tensor_tensor(before[:], before[:], within[:], ALU.add))
            for k in range(2):
                step(v.tensor_tensor(within[:], before[:], hot[k][:], ALU.mult))
                step(v.tensor_reduce(small[3][:], grid(within[:]), AXX, ALU.add))
                step(v.tensor_tensor(grid(totals[:]), grid(hot[k][:]), base, ALU.mult))
                first = xrow[:, :, FIRST] if k == 0 else small[4][:]
                step(v.tensor_reduce(first, grid(totals[:]), AXX, ALU.add))
                step(v.tensor_scalar(small[5][:], small[3][:], float(CAP), FAR_SLOT, ALU.is_gt, ALU.mult))
                step(v.scalar_tensor_tensor(out=small[6][:], in0=small[3][:], scalar=-1.0, in1=first, op0=ALU.add, op1=ALU.add))
                step(v.tensor_tensor(slot[:, k, :], small[6][:], small[5][:], ALU.add))
            v.tensor_copy(small[7][:, 0:1], small[6][:, 0:1]).then_inc(s["slots_ready"], 1)

            for j in range(2):
                for a in range(NA):
                    rowmax(0, j, a)
                if j == 0:
                    neg_max(0, 0)
            sequences(body, dve)
            finish_recip(B - 1)
            for b in range(B):
                if b == B - 1:
                    finish_norm(b)
                    finish_add(b)
                dve.wait_ge(ffn_loaded[b % 2], 16 * (b // 2 + 1))
                dve.wait_ge(s["res_added"], b + 1)
                r = res[:, b * S:(b + 1) * S]
                v.tensor_tensor(r, r, ffn[:, b % 2, :], ALU.add).then_inc(s["ffn_added"], 1)

        @block.gpsimd
        def _(pool):
            p = nc.gpsimd

            def keep_xn(b):
                pool.wait_ge(s["var_ready"], 3 * b + 3)
                at_least(pool, s["xn_ready"], b)
                p.tensor_tensor(rstd[:], vpe[:], nhalf[:], ALU.pow).then_inc(s["rstd_ready"], 1)
                pool.wait_ge(s["xn_ready"], b + 1)
                p.tensor_copy(xrow[:, bass.ds(b * TS, TS), 0:C], xn[:]).then_inc(s["xn_kept"], 1)

            pool.wait_ge(s["sums_init"], 1)
            keep_xn(0)
            with pool.Fori(1, B) as b:
                keep_xn(b)

            def scatter(i):
                if i == 0:
                    pool.wait_ge(s["slots_ready"], 1)
                    pool.wait_ge(s["slots_zeroed"], 16 * E)
                    pool.wait_ge(s["rows_ready"], 16)
                k, t = SCATTERS[i]
                p.indirect_dma_start(slot_rows, bass.IndirectOffsetOnAxis(ap=slot[:, k, t:t + 1], axis=0),
                                     xrow[:, t, :], None, bounds_check=E * CAP - 1, oob_is_err=False).then_inc(s["scattered"], 16)

            def diagonal(cols, unit):
                if len(unit) == 1:
                    return cols[:, 0:P], [[1, P]]
                gap_tiles = unit[1][2] // P
                return cols.rearrange("p (k n) -> p k n", k=TS)[:, 0:gap_tiles + 1:gap_tiles, :], [[0, 2], [1, P]]

            def expert_back(e):
                pool.wait_ge(s["ffn_zeroed"], 16 * (B + 1))
                pool.wait_ge(s["eo_ready_out"], e + 1)
                wait_first(pool, s["pool_passed"], s["eo_added"], 16 * TS * e)
                for t in range(TS):
                    p.indirect_dma_start(ffn_rows, bass.IndirectOffsetOnAxis(ap=back[:, t:t + 1], axis=0),
                                         eo[:, t * C:(t + 1) * C], None, bounds_check=N + CAP - 1, oob_is_err=True,
                                         compute_op=ALU.add).then_inc(s["eo_added"], 16)

            def body(b, experts):
                e = 2 * (b - EXPERT_FROM)
                for j in range(QUADS):
                    g = QUADS * b + j
                    for u, unit in enumerate(UNITS):
                        n = NU * g + u
                        wait_first(pool, s["pool_passed"], s["exp_done"], n + 1)
                        tile, pattern = diagonal(probs[:, j % 2, u * 512:(u + 1) * 512], unit)
                        p.affine_select(out=tile, in_=tile, compare_op=ALU.is_ge, fill=0.0, base=0, pattern=pattern,
                                        channel_multiplier=-1).then_inc(s["probs_masked"], 1)
                        if u == 8:
                            at_least(pool, s["pv_done"], QUADS * (b - 1) + j + 1)
                            wait_first(pool, s["pool_passed"], s["v_copied"], b + 1)
                            p.tensor_scalar(vaug[:, j, :, :, 0:DK], vstage[:, :, 4 * j:4 * j + 4, :], 1.0, 0.0,
                                            ALU.mult, ALU.add).then_inc(s["vaug_ready"], 1)
                        if isinstance(b, int) and b < EXPERT_FROM:
                            for i in range(len(SCATTERS) * n // SPREAD, len(SCATTERS) * (n + 1) // SPREAD):
                                scatter(i)
                        if experts and (j, u) == (2, 5):
                            expert_back(e)
                        if experts and (j, u) == (3, 5):
                            expert_back(e + 1)

            pool.wait_ge(s["init_done"], 4)
            sequences(body, pool)

        @block.scalar
        def _(act):
            a = nc.scalar
            act.dma_start(ident[:], ident_in).then_inc(s["ident_loaded"], 16)
            act.dma_start(bias_rows[0:HJ, :], rb1.rearrange("(j p) -> j p", p=P)).then_inc(s["bias_loaded"], 16)
            act.dma_start(bias_rows[HJ:, :], eb1.rearrange("e (j p) -> (e j) p", p=P)).then_inc(s["bias_loaded"], 16)
            act.dma_start(w1r, rw1).then_inc(s["router_loaded"], 16)
            act.wait_ge(s["w2r_zero"], 1)
            act.dma_start(w2r[:, :, 0:E], rw2.rearrange("(j p) e -> p j e", p=P)).then_inc(s["router_loaded"], 16)
            act.dma_start(b2r[:], rb2.rearrange("(o e) -> o e", o=1).broadcast_to([P, E])).then_inc(s["router_loaded"], 16)
            act.dma_start(sel[:], sel_in).then_inc(s["router_loaded"], 16)
            for dst, src in ((wq, Wq), (wk, Wk), (wv, Wv), (wo, Wo), (cosT, cos_in), (sinT, sin_in), (amask, amask_in)):
                act.dma_start(dst[:], src).then_inc(s["attn_loaded"], 16)
            for dst, src in ((tri, tri_in), (erow, erow_in), (trash, trash_in)):
                act.dma_start(dst[:], src).then_inc(s["route_loaded"], 16)
            act.dma_start(small[7][:], token_in).then_inc(s["route_loaded"], 16)
            act.wait_ge(s["zrow_zero"], 1)
            for e in range(E):
                act.dma_start(slot_rows.rearrange("(e t p) c -> e p t c", p=P, t=TS)[e],
                              zrow[:].rearrange("p (t c) -> p t c", c=ROW)).then_inc(s["slots_zeroed"], 16)
            for i in range(B + 1):
                act.dma_start(ffn_rows.rearrange("(b t p) c -> b p t c", p=P, t=TS)[i],
                              zrow[:, 0:TS * C].rearrange("p (t c) -> p t c", c=C)).then_inc(s["ffn_zeroed"], 16)

            def copy_xnT(b):
                act.wait_ge(s["xnT_ready"], b + 1)
                a.copy(xnT[:, bass.ds(b * S, S)], bank_a[0][:]).then_inc(s["xnT_copied"], 1)

            act.wait_ge(s["biases_ready"], 1)
            a.copy(biases[:], bank_misc[:, 0:HJ * (E + 1)]).then_inc(s["biases_copied"], 1)
            copy_xnT(0)
            act.wait_ge(s["biases_copied"], 1)

            def router(b):
                for h in range(HJ):
                    act.wait_ge(s["hid_ready"], HJ * b + h + 1)
                    if h == 0:
                        at_least(act, s["lgT_ready"], b)
                    a.activation(hid[:, h, :], bank_b[h % 2][:], ACT.Relu, bias=biases[:, h:h + 1]).then_inc(s["hid_relu"], 1)
                if not is_last(b):
                    copy_xnT(b + 1)
                act.wait_ge(s["lgT_ready"], b + 1)
                at_least(act, s["lg_ready"], b)
                a.copy(lgT[:], bank_o[:]).then_inc(s["lgT_copied"], 1)

            router_steps(router, act)

            def part(b, w, k):
                i = 2 * b + w
                if k == 0:
                    act.wait_ge(s["rope_sum"], i + 1)
                    at_least(act, s["qk_stored"], 96 * b)
                    a.copy(parts[:, w, 0, :], qk[:, w, :]).then_inc(s["part1"], 1)
                else:
                    act.wait_ge(s["rest1"], i + 1)
                    a.copy(parts[:, w, 1, :], qk[:, w, :]).then_inc(s["part2"], 1)

            def evict_o(b, j):
                act.wait_ge(s["pv_done"], QUADS * b + j + 1)
                at_least(act, o_stored[j % 2], 16 * (2 * b + j // 2))
                a.copy(osb[:, j % 2, :], bank_o[:]).then_inc(s["o_copied"], 1)

            def turn_rows(e):
                act.wait_ge(s["dT_ready"], e + 1)
                at_least(act, s["eh_ready"], HJ * e)
                a.copy(dspT[:], bank_misc[:]).then_inc(s["dT_copied"], 1)

            def relu(e, h):
                act.wait_ge(s["eh_ready"], HJ * e + h + 1)
                if h == 0:
                    at_least(act, s["eo_ready"], e)
                a.activation(hid[:, h, :], (bank_proj, bank_misc)[h % 2][:], ACT.Relu,
                             bias=biases[:, bass.ds(HJ * e + HJ + h, 1)]).then_inc(s["eh_relu"], 1)

            def body(b, experts):
                last = is_last(b)
                e = 2 * (b - EXPERT_FROM)
                for j in range(QUADS):
                    g = QUADS * b + j
                    for u in range(NU):
                        n = NU * g + u
                        act.wait_ge(s["scores_ready"], n + 1)
                        if u == 0:
                            at_least(act, s["pv_done"], g - 1)
                        a.activation(probs[:, j % 2, u * 512:(u + 1) * 512], bank_b[u % 2][:], ACT.Exp, scale=SCALE).then_inc(s["exp_done"], 1)
                        if j == 0 and u == 7:
                            act.wait_ge(s["v_ready"], b + 1)
                            at_least(act, s["vaug_ready"], QUADS * b)
                            a.copy(vstage[:].rearrange("p t h d -> p (t h d)"), bank_misc[:]).then_inc(s["v_copied"], 1)
                        if not last:
                            if j == 0 and u in (5, 7):
                                part(b + 1, 0, (u - 5) // 2)
                            if j == 0 and u == 9:
                                part(b + 1, 1, 0)
                            if j == 1 and u == 0:
                                part(b + 1, 1, 1)
                        if u == 8:
                            if j > 0:
                                evict_o(b, j - 1)
                            elif begun(b):
                                evict_o(b - 1, 3)
                        if experts and j in (1, 2):
                            if u == 1:
                                turn_rows(e + j - 1)
                            if u in (4, 5, 7, 8):
                                relu(e + j - 1, (4, 5, 7, 8).index(u))

            for w in range(2):
                for k in range(2):
                    part(0, w, k)
            act.wait_ge(s["topped"], TOPS * B)
            a.activation(small[0][:], gap[:], ACT.Exp).then_inc(s["gap_exp"], 1)
            act.wait_ge(s["route_loaded"], 16 * 4)
            act.wait_ge(s["xn_kept"], B)
            a.copy(xrow[:, :, TOKEN], small[7][:]).then_inc(s["rows_ready"], 16)
            act.wait_ge(s["counts_ready"], 1)
            a.copy(within[:], bank_misc[:, 0:NT * E])
            a.copy(totals[:], bank_misc[:, NT * E:2 * NT * E]).then_inc(s["counts_copied"], 1)
            sequences(body, act)
            evict_o(B - 1, 3)

        @block.tensor
        def _(pe):
            t = nc.tensor

            def turn_xn(b):
                pe.wait_ge(s["xn_ready"], b + 1)
                at_least(pe, s["xnT_copied"], b)
                for i in range(TS):
                    ins = t.transpose(bank_a[0][:, i * P:(i + 1) * P], xn[:, i, :], ident[:])
                ins.then_inc(s["xnT_ready"], 1)

            def sum_logits(b):
                pe.wait_ge(s["lgT_copied"], b + 1)
                at_least(pe, s["topped"], TOPS * b)
                for i in range(TS):
                    ins = t.matmul(bank_proj[:, i * E:(i + 1) * E], lgT[:, i * P:(i + 1) * P], sel[:], start=True, stop=True)
                ins.then_inc(s["lg_ready"], 1)

            def router(b):
                for h in range(HJ):
                    if h == 0:
                        pe.wait_ge(s["xnT_copied"], b + 1)
                    at_least(pe, s["hid_relu"], HJ * b + h - 1)
                    t.matmul(bank_b[h % 2][:], w1r[:, h * P:(h + 1) * P], xnT[:, bass.ds(b * S, S)], start=True, stop=True).then_inc(s["hid_ready"], 1)
                    if h == 1 and begun(b):
                        sum_logits(b - 1)
                if not is_last(b):
                    turn_xn(b + 1)
                pe.wait_ge(s["hid_relu"], HJ * b + HJ)
                at_least(pe, s["lgT_copied"], b)
                for h in range(HJ):
                    ins = t.matmul(bank_o[32 * h:32 * h + 32, :], w2r[:, h, :], hid[:, h, :], start=True, stop=True)
                ins.then_inc(s["lgT_ready"], 1)

            pe.wait_ge(s["ident_loaded"], 16)
            pe.wait_ge(s["bias_loaded"], 32)
            t.transpose(bank_misc[:, 0:HJ * (E + 1)], bias_rows[:], ident[0:HJ * (E + 1), 0:HJ * (E + 1)]).then_inc(s["biases_ready"], 1)
            turn_xn(0)
            pe.wait_ge(s["router_loaded"], 16 * 4)
            router_steps(router, pe)

            def project(b, w, k):
                at_least(pe, s["rope_mul"], 4 * b + 2 * w + k)
                if w == 0 and k == 0:
                    at_least(pe, s["eo_biased"], 2 * (b - 1 - EXPERT_FROM))
                t.matmul(bank_proj[:], ((wq, wqr), (wk, wkr))[w][k][:], xnT[:, bass.ds(b * S, S)], start=True, stop=True).then_inc(s["proj_ready"], 1)

            def project_v(b):
                pe.wait_ge(s["xv_loaded"], 16 * b + 16)
                pe.wait_ge(s["negm_ready"], 2 * (QUADS * b + 2))
                for i in range(TS):
                    ins = t.matmul(bank_misc[:, i * P:(i + 1) * P], xv[:, i * P:(i + 1) * P], wv[:], start=True, stop=True)
                ins.then_inc(s["v_ready"], 1)

            def scores_a(b, j, a):
                h, tiles = AUNITS[a]
                g = QUADS * b + j
                before_it = 16 * g + 4 * (a // 3) + (0, 2, 3)[a % 3]
                at_least(pe, s["rowmax_done"], before_it - 4 + (2, 1, 1)[a % 3])
                if a == 0:
                    pe.wait_ge(slot_loaded[j], 48 * (b + 1))
                for qt, c in tiles:
                    ins = t.matmul(bank_a[a % 3][:, c:c + P * (qt + 1)], Q[0:KROWS, j, h, qt * P:(qt + 1) * P],
                                   K[0:KROWS, j, h, 0:P * (qt + 1)], start=True, stop=True)
                ins.then_inc(s["a_ready"], 1)

            def turn_max(b, j):
                g = QUADS * b + j
                pe.wait_ge(s["rowmax_done"], 16 * (g + 1))
                if j == 2:
                    pe.wait_ge(s["v_copied"], b + 1)
                if j == 1:
                    at_least(pe, s["res_added"], b - 1)
                t.transpose(bank_misc[0:16, 0:P], rmax[:, j % 2, :], ident[:]).then_inc(s["mt_ready"], 1)

            def scores_b(b, j, u):
                n = NU * (QUADS * b + j) + u
                at_least(pe, s["exp_done"], n - 1)
                if u == 0:
                    pe.wait_ge(m_loaded[j], 16 * (b + 1))
                for h, kt, c, w in UNITS[u]:
                    ins = t.matmul(bank_b[u % 2][:, c:c + w], K[0:KROWS, j, h, kt * P:(kt + 1) * P], Q[0:KROWS, j, h, kt * P:S],
                                   start=True, stop=True)
                ins.then_inc(s["scores_ready"], 1)

            def weigh_v(b, j, kt):
                g = QUADS * b + j
                if kt == 0:
                    pe.wait_ge(s["probs_masked"], NU * (g + 1))
                    pe.wait_ge(s["vaug_ready"], g + 1)
                    at_least(pe, s["o_copied"], g)
                for h in range(4):
                    at, w = PIECE[h, kt]
                    ins = t.matmul(bank_o[VW * h:VW * h + VW, kt * P:S], vaug[:, j, kt, h, :], probs[:, j % 2, at:at + w],
                                   start=(kt == 0), stop=(kt == TS - 1), skip_group_check=True)
                if kt == TS - 1:
                    ins.then_inc(s["pv_done"], 1)

            def project_o(b, maxima):
                pe.wait_ge(s["on_ready"], b + 1)
                pe.wait_ge(s["negm_ready"], 2 * maxima)
                for i in range(TS):
                    ins = t.matmul(bank_misc[:, i * P:(i + 1) * P], oT[:, i * P:(i + 1) * P], wo[:], start=True, stop=True)
                ins.then_inc(s["out_ready"], 1)

            def expert_turn(e, i, maxima):
                pe.wait_ge(ew_loaded[i], 64 + 32 * (e - i))
                at_least(pe, s["eh_relu"], HJ * e)
                pe.wait_ge(s["negm_ready"], 2 * maxima)
                for k in range(TS):
                    ins = t.transpose(bank_misc[:, k * P:(k + 1) * P], dsp[:, k, 0:C], ident[:])
                ins.then_inc(s["dT_ready"], 1)

            def expert_hidden(e, i, h, maxima):
                if h == 0:
                    pe.wait_ge(s["dT_copied"], e + 1)
                    at_least(pe, s["eo_biased"], e)
                elif h == 1:
                    pe.wait_ge(s["negm_ready"], 2 * maxima)
                else:
                    pe.wait_ge(s["eh_relu"], HJ * e + h - 1)
                t.matmul((bank_proj, bank_misc)[h % 2][:], w1s[:, i, h * P:(h + 1) * P], dspT[:], start=True, stop=True).then_inc(s["eh_ready"], 1)

            def expert_result(e, i, k):
                if k == 0:
                    pe.wait_ge(s["eh_relu"], HJ * e + HJ)
                for h in range(HJ):
                    ins = t.matmul(bank_proj[:, k * P:(k + 1) * P], hid[:, h, k * P:(k + 1) * P], w2s[:, i, h, :],
                                   start=(h == 0), stop=(h == HJ - 1))
                if k == TS - 1:
                    ins.then_inc(s["eo_ready"], 1)

            def body(b, experts):
                last = is_last(b)
                e = 2 * (b - EXPERT_FROM)
                for j in range(QUADS):
                    done = 0
                    turned = QUADS * b + j + 2
                    for u in range(NU):
                        if experts and j == 1 and u == 0:
                            pe.wait_ge(s["v_copied"], b + 1)
                        if experts and j in (1, 2) and u == 0:
                            expert_turn(e + j - 1, j - 1, turned - 1)
                        if experts and j in (1, 2) and u in (3, 4, 6, 7):
                            expert_hidden(e + j - 1, j - 1, (3, 4, 6, 7).index(u), turned)
                        if experts and j in (2, 3) and u < 2:
                            expert_result(e + j - 2, j - 2, 2 * u)
                            expert_result(e + j - 2, j - 2, 2 * u + 1)
                        if j == 0 and not last and u in (0, 2, 4, 6):
                            i = (0, 2, 4, 6).index(u)
                            project(b + 1, i // 2, i % 2)
                        scores_b(b, j, u)
                        for _ in range(A_BESIDE[u]):
                            if j < 2:
                                scores_a(b, j + 2, done)
                            elif not last:
                                scores_a(b + 1, j - 2, done)
                            done += 1
                        if u == 2:
                            if experts and j in (1, 2):
                                pe.wait_ge(s["dT_copied"], e + j)
                            if experts and j in (2, 3):
                                pe.wait_ge(s["eh_relu"], HJ * (e + j - 1))
                            if j < 3:
                                turn_max(b, j + 1)
                            elif not last:
                                turn_max(b + 1, 0)
                        if j == 0 and u == 6:
                            project_v(b)
                        if u in (1, 3, 5, 7):
                            if j > 0:
                                weigh_v(b, j - 1, u // 2)
                            elif begun(b):
                                weigh_v(b - 1, 3, u // 2)
                        if j == 3 and u == 9 and begun(b):
                            project_o(b - 1, QUADS * (b + 1) + (0 if last else 1))

            pe.wait_ge(s["attn_loaded"], 16 * 7)
            pe.wait_ge(s["rotated"], 4)
            sum_logits(B - 1)
            pe.wait_ge(s["topped"], TOPS * (B - 1) + 1)
            for i in range(4):
                project(0, i // 2, i % 2)
            pe.wait_ge(s["biases_copied"], 1)
            pe.wait_ge(s["route_loaded"], 16 * 4)
            pe.wait_ge(s["sums_init"], 2)
            pe.wait_ge(s["picked_ready"], 1)
            t.matmul(bank_misc[:, 0:NT * E], tri[:], picked[:], start=True, stop=True)
            t.matmul(bank_misc[:, NT * E:2 * NT * E], ones[:], picked[:], start=True, stop=True).then_inc(s["counts_ready"], 1)
            pe.wait_ge(s["xnT_copied"], B)
            for j in range(2):
                for a in range(NA):
                    scores_a(0, j, a)
                if j == 0:
                    pe.wait_ge(s["counts_copied"], 1)
                    turn_max(0, 0)
            sequences(body, pe)
            for kt in range(TS):
                weigh_v(B - 1, 3, kt)
            pe.wait_ge(s["res_added"], B - 1)
            project_o(B - 1, QUADS * B)


def constants(B, S, DK, E, CAP):
    import numpy as np
    f = np.float32
    N = B * S
    pos = np.arange(S, dtype=f)
    inv = (f(1.0) / np.power(f(10000.0), np.arange(0, DK, 2, dtype=f) / f(DK))).astype(f)
    angles = np.outer(pos, inv).astype(f)
    cos = np.repeat(np.cos(angles), 2, axis=-1).astype(f)
    sin = np.repeat(np.sin(angles), 2, axis=-1).astype(f)
    q = np.arange(P)
    amask = np.zeros((P, S), f)
    amask[:, S - P:] = np.where(q[None, :] <= q[:, None], 0.0, -BIG)
    sel = np.zeros((P, E), f)
    for h in range(4):
        sel[32 * h + np.arange(E), np.arange(E)] = 1.0
    erow = np.concatenate([E - np.arange(E), CAP * np.arange(E)]).astype(f)
    token = (q[:, None] + P * np.arange(N // P)[None, :]).astype(f)
    return {
        "ident": np.eye(P, dtype=f),
        "cosT": np.ascontiguousarray(np.tile(cos.T, (HEADS, 1))),
        "sinT": np.ascontiguousarray(np.tile(sin.T, (HEADS, 1))),
        "amask": amask,
        "tri": (q[:, None] <= q[None, :]).astype(f),
        "sel": sel,
        "erow": np.ascontiguousarray(np.tile(erow, (P, 1))),
        "token": np.ascontiguousarray(token + f(1.0)),
        "trash": np.ascontiguousarray(token[:, 0:S // P] + f(N + 1)),
        "zeros": np.zeros((2, 2 * S), f),
    }


_INS = ["L0_attn_x", "L0_attn_Wq", "L0_attn_Wk", "L0_attn_Wv", "L0_attn_Wo", "L0_ffn_rw1", "L0_ffn_rb1",
        "L0_ffn_rw2", "L0_ffn_rb2", "L0_ffn_ew1", "L0_ffn_eb1", "L0_ffn_ew2", "L0_ffn_eb2"]


def kernel(**inputs):
    import numpy as _np
    import concourse.bacc as _bacc
    from concourse import mybir as _mybir
    from concourse.bass_utils import run_bass_kernel_spmd as _run

    nc = _bacc.Bacc("TRN2", target_bir_lowering=False, num_devices=1)
    B, S, C = inputs["L0_attn_x"].shape
    E = inputs["L0_ffn_ew1"].shape[0]
    arrays, args = {}, []
    named = {n: _np.ascontiguousarray(inputs[n]) for n in _INS}
    named.update(constants(B, S, C // HEADS, E, S))
    for name, a in named.items():
        arrays[f"in_{name}_dram"] = a
        args.append(nc.dram_tensor(f"in_{name}_dram", a.shape, _mybir.dt.from_np(a.dtype), kind="ExternalInput").ap())
    args.append(nc.dram_tensor("out_0_dram", (B, S, C), F32, kind="ExternalOutput").ap())
    build(nc, *args)
    r = _run(nc, [arrays], core_ids=[0])
    return r.results[0]["out_0_dram"]
```

```python
from contextlib import ExitStack

import concourse.bass as bass
from concourse import mybir

F32 = mybir.dt.float32
BF16 = mybir.dt.bfloat16
U32 = mybir.dt.uint32
ALU = mybir.AluOpType
ACT = mybir.ActivationFunctionType
AXX = mybir.AxisListType.X

P = 128
HEADS = 16
PARTS = 3
TERMS = PARTS * PARTS
EPS = 1e-5
BIG = 3.0e38
FAR_SLOT = 65536.0
ROW = 132
TOKEN, FIRST, GAP, SECOND = 128, 129, 130, 131
EXPERT_FROM = 3


def at_least(eng, sem, value):
    if not isinstance(value, int) or value > 0:
        eng.wait_ge(sem, value)


def wait_first(eng, passed, sem, value):
    at_least(eng, sem, value)
    if not isinstance(value, int):
        eng.sem_inc(passed, 1)


def build(nc, x, Wq, Wk, Wv, Wo, rw1, rb1, rw2, rb2, ew1, eb1, ew2, eb2,
          ident_in, cos_in, sin_in, amask_in, tri_in, sel_in, erow_in, token_in, trash_in, zeros_in, out):
    B, S, C = x.shape
    E, _, H = ew1.shape
    CAP = S
    N = B * S
    NT = N // P
    TS = S // P
    HJ = H // P
    DK = C // HEADS
    QUADS = HEADS // 4
    MROW = TERMS * DK
    KROWS = 96
    SCALE = float(DK) ** -0.5
    VW = 32
    TOPS = 13
    WEIGH_STEPS = 6
    assert (C, S, TS, QUADS, HJ) == (P, 512, 4, 4, 4) and 2 * (B - 1 - EXPERT_FROM) == E

    PAIR_UNITS = [[(0, 0, 0, 512)], [(0, 1, 0, 384), (0, 3, 384, 128)],
                  [(1, 0, 0, 512)], [(1, 1, 0, 384), (1, 3, 384, 128)],
                  [(0, 2, 0, 256), (1, 2, 256, 256)]]
    UNITS = [[(2 * i + h, kt, c, n) for h, kt, c, n in unit] for i in range(2) for unit in PAIR_UNITS]
    NU = len(UNITS)
    PIECE = {(h, kt): (u * 512 + c, n) for u, unit in enumerate(UNITS) for h, kt, c, n in unit}
    AUNITS = [(h, tiles) for h in range(4) for tiles in ([(0, 0), (1, P)], [(2, 0)], [(3, 0)])]
    NA = len(AUNITS)
    A_BESIDE = [2, 1, 1, 1, 1, 2, 1, 1, 1, 1]
    SCATTERS = [(k, t) for k in range(2) for t in range(NT)]
    SCATTER_FROM = 2 * NU - 2
    FFN_AT = [(2, 1), (2, 4), (2, 9), (3, 1), (3, 9), (3, 10)]
    SPREAD = EXPERT_FROM * QUADS * NU - SCATTER_FROM

    slot_rows = nc.dram_tensor("slot_rows", (E * CAP, ROW), F32, kind="Internal").ap()
    ffn_rows = nc.dram_tensor("ffn_rows", (N + CAP, C), F32, kind="Internal").ap()
    qk_dram = nc.dram_tensor("qk_dram", (B * 2 * P, TERMS * S), BF16, kind="Internal").ap()
    m_dram = nc.dram_tensor("m_dram", (B * QUADS * 16, 2 * P), BF16, kind="Internal").ap()
    o_dram = nc.dram_tensor("o_dram", (B * QUADS * P, S), F32, kind="Internal").ap()
    oc_dram = nc.dram_tensor("oc_dram", (B * P, S), F32, kind="Internal").ap()
    d_dram = nc.dram_tensor("d_dram", (B * HEADS, S), F32, kind="Internal").ap()
    rb_dram = nc.dram_tensor("rb_dram", (B * P, S), F32, kind="Internal").ap()
    r_dram = nc.dram_tensor("r_dram", (B * HEADS, S), F32, kind="Internal").ap()

    with ExitStack() as ctx:
        def sb(name, shape, dt=F32):
            return ctx.enter_context(nc.sbuf_tensor(name, shape, dt))

        def sem(name):
            return ctx.enter_context(nc.semaphore(name))

        banks = [ctx.enter_context(nc.psum_tensor(f"bank{i}", [P, 512], F32)) for i in range(8)]
        bank_a = banks[0:3]
        bank_b = banks[3:5]
        bank_o = banks[5]
        bank_proj = banks[6]
        bank_misc = banks[7]

        ident = sb("ident", [P, P])
        cosT = sb("cosT", [P, S])
        sinT = sb("sinT", [P, S])
        amask = sb("amask", [P, S])
        tri = sb("tri", [P, P])
        ones = sb("ones", [P, P])
        sel = sb("sel", [P, E])
        erow = sb("erow", [P, 2 * E])
        trash = sb("trash", [P, TS])
        wq = sb("wq", [P, C])
        wk = sb("wk", [P, C])
        wqr = sb("wqr", [P, C])
        wkr = sb("wkr", [P, C])
        wv = sb("wv", [P, C])
        wo = sb("wo", [P, C])
        bias_rows = sb("bias_rows", [HJ * (E + 1), P])
        biases = sb("biases", [P, HJ * (E + 1)])
        w2r = sb("w2r", [P, HJ, 32])
        b2r = sb("b2r", [P, E])
        res = sb("res", [P, NT * C])
        xrow = sb("xrow", [P, NT, ROW])
        xnT = sb("xnT", [P, N])
        stats = sb("stats", [P, TS, 6])
        mv = sb("mv", [P, TS, 2])
        vpe = sb("vpe", [P, TS])
        nhalf = sb("nhalf", [P, TS])
        rstd = sb("rstd", [P, TS])
        hid = sb("hid", [P, HJ, S])
        lgT = sb("lgT", [P, S])
        dspT = lgT
        lg = [sb(f"lg{i}", [P, TS * E]) for i in range(4)]
        top = [sb(f"top{i}", [P, TS]) for i in range(3)]
        hot = [sb(f"hot{k}", [P, NT * E]) for k in range(2)]
        picked = sb("picked", [P, NT * E])
        within = sb("within", [P, NT * E])
        totals = sb("totals", [P, NT * E])
        before = sb("before", [P, NT * E])
        gap = sb("gap", [P, NT])
        small = [sb(f"small{i}", [P, NT]) for i in range(8)]
        slot = sb("slot", [P, 2, NT], U32)
        w1s = sb("w1s", [P, 2, H])
        w1r = w1s[:, 0]
        w2s = sb("w2s", [P, 2, HJ, C])
        b2s = sb("b2s", [P, 2, C])
        dsp = sb("dsp", [P, 2, TS, ROW])
        xn = dsp[:, 1, :, 0:C]
        ew = [sb(f"ew{i}", [P, 2, TS]) for i in range(5)]
        back = sb("back", [P, 2, TS], U32)
        eo = sb("eo", [P, TS * C])
        xv = sb("xv", [P, S])
        rope = sb("rope", [P, 4, S])
        qk = sb("qk", [P, 2, S])
        parts = sb("parts", [P, 2, PARTS, S], BF16)
        Q = sb("Q", [P, QUADS, 4, S], BF16)
        K = sb("K", [P, QUADS, 4, S], BF16)
        rmax = sb("rmax", [P, 2, 16])
        negm = sb("negm", [16, 2, P], BF16)
        probs = sb("probs", [P, 2, NU * 512])
        vstage = sb("vstage", [P, TS, HEADS, DK])
        vaug = sb("vaug", [P, QUADS, TS, 4, VW])
        osb = sb("osb", [P, 2, S])
        oT = sb("oT", [P, S])
        dcomp = sb("dcomp", [P, 64])
        rcomp = sb("rcomp", [P, 64])
        rbc = sb("rbc", [P, S])
        zrow = sb("zrow", [P, TS * ROW])
        o_rec = sb("o_rec", [P, TS * 4])
        otok = eo
        ffn = rope

        s = {}
        for name in """ident_loaded bias_loaded router_loaded route_loaded attn_loaded x_loaded w2r_zero zrow_zero
            sums_init rows_set ones_set rotated
            var_ready rstd_ready xn_ready xn_kept xnT_ready xnT_copied hid_ready hid_relu lgT_ready lgT_copied
            lg_ready topped biases_ready biases_copied picked_ready counts_ready counts_copied gap_exp
            route slots_ready rows_ready slots_zeroed ffn_zeroed scattered
            xv_loaded v_ready v_copied vaug_ready proj_ready rope_mul rope_sum part1 rest1 part2 part3
            qk_stored a_ready rowmax_done mt_ready negm_ready m_stored scores_ready exp_done probs_masked
            pv_done o_copied d_closed o_closed d_loaded o_loaded rec_ready rec_stored rec_spread rbc_loaded
            on_ready out_ready res_added
            dT_ready dT_copied eh_ready eh_relu eo_ready eo_biased eo_ready_out eo_added weighing
            ffn_added out_stored o_turned o_recip o_scaled ot_ready ot_copied dve_passed pool_passed""".split():
            s[name] = sem(name)
        slot_loaded = [sem(f"slot_loaded{j}") for j in range(QUADS)]
        m_loaded = [sem(f"m_loaded{j}") for j in range(QUADS)]
        o_stored = [sem(f"o_stored{p}") for p in range(2)]
        ew_loaded = [sem(f"ew_loaded{i}") for i in range(2)]
        ffn_loaded = [sem(f"ffn_loaded{i}") for i in range(2)]

        block = ctx.enter_context(nc.Block())

        def begun(b):
            return not (isinstance(b, int) and b == 0)

        def sequences(body, eng):
            for b in range(EXPERT_FROM + 1):
                body(b, b >= EXPERT_FROM)
            with eng.Fori(EXPERT_FROM + 1, B - 1) as b:
                body(b, True)
            body(B - 1, False)

        def is_last(b):
            return isinstance(b, int) and b == B - 1

        @block.sync
        def _(sp):
            xt = x.rearrange("b (t p) c -> p (b t) c", p=P)
            ot = out.rearrange("b (t p) c -> p (b t) c", p=P)
            rest = res[:].rearrange("p (t c) -> p t c", c=C)

            def load_x(b):
                at_least(sp, s["x_loaded"], 16 * b)
                sp.dma_start(rest[:, bass.ds(b * TS, TS), :], xt[:, bass.ds(b * TS, TS), :]).then_inc(s["x_loaded"], 16)

            load_x(0)
            for dst, src in ((wq, Wq), (wk, Wk), (cosT, cos_in), (sinT, sin_in), (wv, Wv), (wo, Wo), (amask, amask_in)):
                sp.dma_start(dst[:], src).then_inc(s["attn_loaded"], 16)
            load_x(1)
            for dst, src in ((erow, erow_in), (tri, tri_in), (trash, trash_in), (small[7], token_in)):
                sp.dma_start(dst[:], src).then_inc(s["route_loaded"], 16)
            with sp.Fori(2, B) as b:
                load_x(b)
            sp.wait_ge(s["zrow_zero"], 1)
            with sp.Fori(0, E) as e:
                sp.dma_start(slot_rows[bass.ds(e * CAP, CAP), :].rearrange("(t p) c -> p t c", p=P),
                             zrow[:].rearrange("p (t c) -> p t c", c=ROW)).then_inc(s["slots_zeroed"], 16)
            with sp.Fori(0, B + 1) as b:
                sp.dma_start(ffn_rows[bass.ds(b * S, S), :].rearrange("(t p) c -> p t c", p=P),
                             zrow[:, 0:TS * C].rearrange("p (t c) -> p t c", c=C)).then_inc(s["ffn_zeroed"], 16)

            def store_parts(b, w):
                sp.wait_ge(s["part3"], 2 * b + w + 1)
                dst = qk_dram[bass.ds((2 * b + w) * P, P), :].rearrange("p (i j n) -> p i j n", i=PARTS, j=PARTS)
                for r in range(PARTS):
                    sp.dma_start(dst[:, :, r, :] if w == 0 else dst[:, r, :, :], parts[:, w]).then_inc(s["qk_stored"], 16)

            def load_slot(b, j):
                sp.wait_ge(s["qk_stored"], 96 * b + 96)
                for w, dst in ((0, Q), (1, K)):
                    src = qk_dram[bass.ds((2 * b + w) * P + j * 4 * DK, 4 * DK), :].rearrange("(h d) (t n) -> (d t) h n", d=DK, t=TERMS)
                    sp.dma_start(dst[0:MROW, j], src).then_inc(slot_loaded[j], 16)
                sp.dma_start(Q[MROW:MROW + 2, j].rearrange("p h n -> p (h n)").bitcast(F32), zeros_in).then_inc(slot_loaded[j], 16)

            def next_slot(b, j):
                sp.wait_ge(s["scores_ready"], NU * (QUADS * b + j + 1))
                load_slot(b + 1, j)

            def store_o(b, j):
                g = QUADS * b + j
                sp.wait_ge(s["o_copied"], g + 1)
                sp.dma_start(o_dram[bass.ds(g * P, P), :], osb[:, j % 2, :]).then_inc(o_stored[j % 2], 16)

            def finish_gather(b):
                for p in range(2):
                    sp.wait_ge(o_stored[p], 16 * (2 * b + 2))
                od = o_dram[bass.ds(b * QUADS * P, QUADS * P), :].rearrange("(h r) n -> h r n", r=VW)
                sp.dma_start(d_dram[bass.ds(b * HEADS, HEADS), :], od[:, DK, :]).then_inc(s["d_closed"], 16)
                sp.dma_start(oc_dram[bass.ds(b * P, P), :].rearrange("(h d) n -> h d n", d=DK), od[:, 0:DK, :]).then_inc(s["o_closed"], 16)

            def finish_loads(b):
                sp.wait_ge(s["d_closed"], 16 * b + 16)
                sp.dma_start(dcomp[:], d_dram[bass.ds(b * HEADS, HEADS), :].rearrange("h (a n) -> (h a) n", n=64)).then_inc(s["d_loaded"], 16)
                sp.wait_ge(s["o_closed"], 16 * b + 16)
                at_least(sp, s["out_ready"], b)
                sp.dma_start(oT[:], oc_dram[bass.ds(b * P, P), :]).then_inc(s["o_loaded"], 16)

            def store_recip(b):
                sp.wait_ge(s["rec_ready"], b + 1)
                sp.dma_start(r_dram[bass.ds(b * HEADS, HEADS), :].rearrange("h (a n) -> (h a) n", n=64), rcomp[:]).then_inc(s["rec_stored"], 16)

            def spread_recip(b):
                sp.wait_ge(s["rec_stored"], 16 * b + 16)
                src = r_dram[bass.ds(b * HEADS, HEADS), :].rearrange("h (o n) -> h o n", o=1).broadcast_to([HEADS, DK, S])
                sp.dma_start(rb_dram[bass.ds(b * P, P), :].rearrange("(h d) n -> h d n", d=DK), src).then_inc(s["rec_spread"], 16)

            def load_recip(b):
                sp.wait_ge(s["rec_spread"], 16 * b + 16)
                at_least(sp, s["on_ready"], b)
                sp.dma_start(rbc[:], rb_dram[bass.ds(b * P, P), :]).then_inc(s["rbc_loaded"], 16)

            def load_xv(b):
                at_least(sp, s["v_ready"], b)
                sp.dma_start(xv[:], xnT[:, bass.ds(b * S, S)]).then_inc(s["xv_loaded"], 16)

            def load_expert(e, i):
                if i == 0:
                    sp.wait_ge(s["scattered"], 16 * 2 * NT)
                at_least(sp, s["eo_biased"], e - 1)
                sp.dma_start(dsp[:, i], slot_rows[bass.ds(e * CAP, CAP), :].rearrange("(t p) c -> p t c", p=P)).then_inc(ew_loaded[i], 16)
                sp.dma_start(w1s[:, i], ew1.rearrange("e c h -> (e c) h")[bass.ds(e * C, C), :]).then_inc(ew_loaded[i], 16)
                sp.dma_start(w2s[:, i], ew2.rearrange("e h c -> (e h) c")[bass.ds(e * H, H), :].rearrange("(j p) c -> p j c", p=P)).then_inc(ew_loaded[i], 16)
                sp.dma_start(b2s[:, i], eb2[bass.ds(e, 1), :].broadcast_to([P, C])).then_inc(ew_loaded[i], 16)

            def load_ffn(b):
                at_least(sp, s["ffn_added"], b - 1)
                sp.dma_start(ffn[:, b % 2, :].rearrange("p (t c) -> p t c", c=C),
                             ffn_rows[b * S:(b + 1) * S, :].rearrange("(t p) c -> p t c", p=P)).then_inc(ffn_loaded[b % 2], 16)

            def store_out(b):
                sp.wait_ge(s["ffn_added"], b + 1)
                sp.wait_ge(s["res_added"], b + 1)
                sp.dma_start(ot[:, b * TS:(b + 1) * TS, :], rest[:, b * TS:(b + 1) * TS, :]).then_inc(s["out_stored"], 16)

            def body(b, experts):
                last = is_last(b)
                e = 2 * (b - EXPERT_FROM)
                load_xv(b)
                if begun(b):
                    next_slot(b - 1, 3)
                else:
                    load_slot(b, 3)
                if experts:
                    load_expert(e, 0)
                if not last:
                    store_parts(b + 1, 0)
                if begun(b):
                    store_o(b - 1, 3)
                if not last:
                    store_parts(b + 1, 1)
                if begun(b):
                    finish_gather(b - 1)
                if not last:
                    next_slot(b, 0)
                if experts:
                    load_expert(e + 1, 1)
                if begun(b):
                    finish_loads(b - 1)
                if last:
                    sp.wait_ge(s["eo_added"], 16 * TS * E)
                    sp.wait_ge(s["rope_sum"], 2 * B)
                    load_ffn(0)
                    load_ffn(1)
                else:
                    store_o(b, 0)
                if not last:
                    next_slot(b, 1)
                if begun(b):
                    store_recip(b - 1)
                    spread_recip(b - 1)
                if last:
                    load_ffn(2)
                    load_ffn(3)
                else:
                    store_o(b, 1)
                if begun(b):
                    load_recip(b - 1)
                if not last:
                    next_slot(b, 2)
                    store_o(b, 2)

            sp.wait_ge(s["rows_set"], 4)
            store_parts(0, 0)
            store_parts(0, 1)
            for j in range(3):
                load_slot(0, j)
            sequences(body, sp)
            for b in range(B):
                if 4 <= b + 2 < B:
                    load_ffn(b + 2)
                store_out(b)
            sp.wait_ge(s["out_stored"], 16 * B)

        @block.vector
        def _(dve):
            v = nc.vector
            v.memset(w2r[:], 0.0).then_inc(s["w2r_zero"], 1)
            v.memset(zrow[:], 0.0).then_inc(s["zrow_zero"], 1)
            v.memset(nhalf[:], -0.5).then_inc(s["sums_init"], 1)

            def rows_of(b):
                return res[:, bass.ds(b * TS * C, TS * C)].rearrange("p (t c) -> p t c", c=C)

            def moments(b):
                dve.wait_ge(s["x_loaded"], 16 * b + 16)
                xs = rows_of(b)
                for t in range(TS):
                    ins = v.bn_stats(stats[:, t, :], xs[:, t, :])
                ins.then_inc(s["var_ready"], 1)
                wait_first(dve, s["dve_passed"], s["var_ready"], 3 * b + 1)
                for t in range(TS):
                    ins = v.bn_aggr(mv[:, t, :], stats[:, t, :])
                ins.then_inc(s["var_ready"], 1)
                dve.wait_ge(s["var_ready"], 3 * b + 2)
                v.tensor_scalar(vpe[:], mv[:, :, 1], EPS, None, ALU.add).then_inc(s["var_ready"], 1)

            def normalise(b):
                xs = rows_of(b)
                dve.wait_ge(s["rstd_ready"], b + 1)
                at_least(dve, s["xnT_ready"], b)
                at_least(dve, s["xn_kept"], b)
                for t in range(TS):
                    ins = v.tensor_scalar(xn[:, t, :], xs[:, t, :], mv[:, t, 0:1], rstd[:, t:t + 1], ALU.subtract, ALU.mult)
                ins.then_inc(s["xn_ready"], 1)

            def grid(a):
                return a.rearrange("p (t e) -> p t e", e=E)

            def wide(a, tiles):
                return a.rearrange("p (t o) -> p t o", o=1).broadcast_to([P, tiles, E])

            def per_expert(a, tiles):
                return a.rearrange("p (o e) -> p o e", o=1).broadcast_to([P, tiles, E])

            def top_two(b):
                n = TOPS * b

                def next_step(ins, k):
                    ins.then_inc(s["topped"], 1)
                    dve.wait_ge(s["topped"], n + k)

                cols = bass.ds(b * TS * E, TS * E)
                pref = per_expert(erow[:, 0:E], TS)
                dve.wait_ge(s["lg_ready"], b + 1)
                next_step(v.tensor_tensor(grid(lg[0][:]), grid(bank_proj[:, 0:TS * E]), per_expert(b2r[:], TS), ALU.add), 1)
                for k in range(2):
                    cur, i = (lg[0], 1) if k == 0 else (lg[3], 7)
                    next_step(v.tensor_reduce(top[k][:], grid(cur[:]), AXX, ALU.max), i + 1)
                    next_step(v.tensor_tensor(grid(lg[1][:]), grid(cur[:]), wide(top[k][:], TS), ALU.is_equal), i + 2)
                    next_step(v.tensor_tensor(grid(lg[2][:]), grid(lg[1][:]), pref, ALU.mult), i + 3)
                    next_step(v.tensor_reduce(top[2][:], grid(lg[2][:]), AXX, ALU.max), i + 4)
                    next_step(v.tensor_tensor(grid(hot[k][:, cols]), grid(lg[2][:]), wide(top[2][:], TS), ALU.is_equal), i + 5)
                    if k == 0:
                        next_step(v.scalar_tensor_tensor(out=lg[3][:], in0=hot[0][:, cols], scalar=-BIG, in1=lg[0][:],
                                                         op0=ALU.mult, op1=ALU.add), 7)
                next_step(v.tensor_tensor(gap[:, bass.ds(b * TS, TS)], top[1][:], top[0][:], ALU.subtract), TOPS)

            def router(b):
                if not is_last(b):
                    normalise(b + 1)
                    if not (isinstance(b, int) and b == B - 2):
                        moments(b + 2)
                if begun(b):
                    top_two(b - 1)

            moments(0)
            normalise(0)
            moments(1)
            v.memset(ones[:], 1.0).then_inc(s["sums_init"], 1)
            router(0)
            dve.wait_ge(s["route_loaded"], 16 * 4)
            dve.wait_ge(s["router_loaded"], 16 * 4)
            dve.wait_ge(s["attn_loaded"], 16 * 7)
            for w, wr in ((wq, wqr), (wk, wkr)):
                src = w[:].rearrange("p (i k) -> p i k", k=2)
                dst = wr[:].rearrange("p (i k) -> p i k", k=2)
                v.tensor_scalar(dst[:, :, 0], src[:, :, 1], -1.0, None, ALU.mult).then_inc(s["rotated"], 1)
                v.tensor_copy(dst[:, :, 1], src[:, :, 0]).then_inc(s["rotated"], 1)

            def ropes(b, w, k, bank=bank_proj):
                dve.wait_ge(s["proj_ready"], 4 * b + 2 * w + k + 1)
                at_least(dve, s["rope_sum"], 2 * (b - 1) + w + 1)
                v.tensor_tensor(rope[:, 2 * w + k, :], bank[:], (cosT if k == 0 else sinT)[:], ALU.mult).then_inc(s["rope_mul"], 1)

            def split(b, w, k):
                i = 2 * b + w
                if k == 0:
                    dve.wait_ge(s["rope_mul"], 2 * i + 2)
                    at_least(dve, s["part3"], i - 1)
                    v.tensor_tensor(qk[:, w, :], rope[:, 2 * w, :], rope[:, 2 * w + 1, :], ALU.add).then_inc(s["rope_sum"], 1)
                elif k == 1:
                    dve.wait_ge(s["part1"], i + 1)
                    v.tensor_tensor(qk[:, w, :], qk[:, w, :], parts[:, w, 0, :], ALU.subtract).then_inc(s["rest1"], 1)
                else:
                    dve.wait_ge(s["part2"], i + 1)
                    v.tensor_tensor(parts[:, w, 2, :], qk[:, w, :], parts[:, w, 1, :], ALU.subtract).then_inc(s["part3"], 1)

            def rowmax(b, j, a):
                h, tiles = AUNITS[a]
                g = QUADS * b + j
                bank = bank_a[a % 3]
                if a == 0:
                    at_least(dve, s["mt_ready"], g - 1)
                wait_first(dve, s["dve_passed"], s["a_ready"], NA * g + a + 1)
                for qt, c in tiles:
                    n = P * (qt + 1)
                    v.tensor_tensor_reduce(bank[:, c:c + n], bank[:, c:c + n], amask[:, S - n:S], 1.0, -BIG, ALU.add, ALU.max,
                                           rmax[:, j % 2, 4 * h + qt:4 * h + qt + 1]).then_inc(s["rowmax_done"], 1)

            def neg_max(b, j):
                g = QUADS * b + j
                dve.wait_ge(s["mt_ready"], g + 1)
                at_least(dve, s["m_stored"], 16 * g)
                v.tensor_scalar(negm[:, 0, :], bank_misc[0:16, 0:P], -1.0, None, ALU.mult).then_inc(s["negm_ready"], 1)
                dve.wait_ge(s["negm_ready"], 2 * g + 1)
                v.scalar_tensor_tensor(out=negm[:, 1, :], in0=bank_misc[0:16, 0:P], scalar=-1.0, in1=negm[:, 0, :],
                                       op0=ALU.mult, op1=ALU.subtract).then_inc(s["negm_ready"], 1)

            def finish_recip(b):
                dve.wait_ge(s["d_loaded"], 16 * b + 16)
                at_least(dve, s["rec_stored"], 16 * b)
                v.reciprocal(rcomp[:], dcomp[:]).then_inc(s["rec_ready"], 1)

            def finish_norm(b):
                dve.wait_ge(s["o_loaded"], 16 * b + 16)
                dve.wait_ge(s["rbc_loaded"], 16 * b + 16)
                v.tensor_tensor(oT[:], oT[:], rbc[:], ALU.mult).then_inc(s["on_ready"], 1)

            def finish_add(b):
                dve.wait_ge(s["out_ready"], b + 1)
                if is_last(b):
                    dve.wait_ge(s["ffn_added"], B)
                r = res[:, bass.ds(b * S, S)]
                v.tensor_tensor(r, bank_misc[:], r, ALU.add).then_inc(s["res_added"], 1)

            def add_ffn(b):
                dve.wait_ge(ffn_loaded[b % 2], 16 * (b // 2 + 1))
                at_least(dve, s["res_added"], min(b, B - 2) + 1)
                r = res[:, b * S:(b + 1) * S]
                v.tensor_tensor(r, r, ffn[:, b % 2, :], ALU.add).then_inc(s["ffn_added"], 1)

            def scale_o(j):
                turned = bank_a[j % 3][:].rearrange("p (t h r) -> p t h r", t=TS, h=4)
                rec = o_rec[:].rearrange("p (t h r) -> p t h r", t=TS, h=4)
                dve.wait_ge(s["o_turned"], j + 1)
                at_least(dve, s["o_scaled"], j)
                v.reciprocal(rec, turned[:, :, :, DK:DK + 1]).then_inc(s["o_recip"], 1)
                dve.wait_ge(s["o_recip"], j + 1)
                if j == 0:
                    dve.wait_ge(s["eo_added"], 16 * TS * E)
                v.tensor_tensor(otok[:].rearrange("p (t h d) -> p t h d", t=TS, h=HEADS)[:, :, 4 * j:4 * j + 4, :],
                                turned[:, :, :, 0:DK], rec.broadcast_to([P, TS, 4, DK]), ALU.mult).then_inc(s["o_scaled"], 1)

            def weigh(e, i):
                dve.wait_ge(ew_loaded[i], 32 * (e - i) + 64)
                n = WEIGH_STEPS * e

                def next_step(ins, k):
                    ins.then_inc(s["weighing"], 1)
                    dve.wait_ge(s["weighing"], n + k)

                row = dsp[:, i]
                is_first, gained, empty, spare, weight = (x[:, i] for x in ew)
                first = erow[:, bass.ds(E + e, 1)]
                at_least(dve, s["eo_added"], 16 * TS * (e - 1))
                next_step(v.tensor_scalar(is_first, row[:, :, FIRST], first, None, ALU.is_equal), 1)
                next_step(v.tensor_tensor(gained, is_first, row[:, :, GAP], ALU.mult), 2)
                next_step(v.tensor_scalar(empty, row[:, :, TOKEN], 0.0, None, ALU.is_equal), 3)
                next_step(v.tensor_tensor(spare, empty, trash[:], ALU.mult), 4)
                next_step(v.tensor_tensor(weight, gained, row[:, :, SECOND], ALU.add), 5)
                next_step(v.scalar_tensor_tensor(out=back[:, i], in0=row[:, :, TOKEN], scalar=-1.0, in1=spare,
                                                 op0=ALU.add, op1=ALU.add), 6)

            def expert_out(e, i):
                tc = "p (t c) -> p t c"
                dve.wait_ge(s["eo_ready"], e + 1)
                at_least(dve, s["eo_added"], 16 * TS * e)
                v.tensor_tensor(eo[:].rearrange(tc, c=C), bank_proj[:].rearrange(tc, c=C),
                                b2s[:, i].rearrange("p (o c) -> p o c", o=1).broadcast_to([P, TS, C]), ALU.add).then_inc(s["eo_biased"], 1)
                dve.wait_ge(s["eo_biased"], e + 1)
                v.tensor_tensor(eo[:].rearrange(tc, c=C), eo[:].rearrange(tc, c=C),
                                ew[4][:, i].rearrange("p (t o) -> p t o", o=1).broadcast_to([P, TS, C]), ALU.mult).then_inc(s["eo_ready_out"], 1)

            count = [0]

            def step(ins):
                count[0] += 1
                ins.then_inc(s["route"], 1)
                dve.wait_ge(s["route"], count[0])

            def route_weights():
                dve.wait_ge(s["gap_exp"], 1)
                step(v.tensor_scalar(small[1][:], small[0][:], 1.0, None, ALU.add))
                step(v.reciprocal(small[2][:], small[1][:]))
                step(v.tensor_tensor(xrow[:, :, SECOND], small[0][:], small[2][:], ALU.mult))
                step(v.tensor_tensor(xrow[:, :, GAP], small[2][:], xrow[:, :, SECOND], ALU.subtract))

            def route_places():
                dve.wait_ge(s["counts_copied"], 1)
                for e in range(E):
                    ins = v.tensor_tensor_scan(grid(before[:])[:, :, e], grid(totals[:])[:, :, e], zrow[:, 0:NT], 0.0, ALU.add, ALU.add)
                step(ins)
                step(v.tensor_tensor(before[:], before[:], totals[:], ALU.subtract))
                step(v.tensor_tensor(before[:], before[:], within[:], ALU.add))

            def route_slots(k):
                step(v.tensor_tensor(within[:], before[:], hot[k][:], ALU.mult))
                step(v.tensor_reduce(small[3][:], grid(within[:]), AXX, ALU.add))
                step(v.tensor_tensor(grid(totals[:]), grid(hot[k][:]), per_expert(erow[:, E:2 * E], NT), ALU.mult))
                first = xrow[:, :, FIRST] if k == 0 else small[4][:]
                step(v.tensor_reduce(first, grid(totals[:]), AXX, ALU.add))
                step(v.tensor_scalar(small[5][:], small[3][:], float(CAP), FAR_SLOT, ALU.is_gt, ALU.mult))
                step(v.scalar_tensor_tensor(out=small[6][:], in0=small[3][:], scalar=-1.0, in1=first, op0=ALU.add, op1=ALU.add))
                v.tensor_tensor(slot[:, k, :], small[6][:], small[5][:], ALU.add).then_inc(s["slots_ready"], 1)

            def body(b, experts):
                last = is_last(b)
                e = 2 * (b - EXPERT_FROM)
                for j in range(QUADS):
                    for a in range(NA):
                        if j < 2:
                            rowmax(b, j + 2, a)
                        elif not last:
                            rowmax(b + 1, j - 2, a)
                        if a == 2 and j < 3:
                            neg_max(b, j + 1)
                        elif a == 2 and not last:
                            neg_max(b + 1, 0)
                        if j == 0 and not last:
                            if a in (1, 3, 7, 9):
                                i = (1, 3, 7, 9).index(a)
                                ropes(b + 1, i // 2, i % 2)
                            if a in (4, 6, 8):
                                split(b + 1, 0, a // 2 - 2)
                            if a in (9, 11):
                                split(b + 1, 1, (a - 9) // 2)
                        if j == 1 and a == 1 and not last:
                            split(b + 1, 1, 2)
                        if last:
                            if (j, a) in FFN_AT:
                                add_ffn(FFN_AT.index((j, a)))
                            if j > 1 and a == 2:
                                scale_o(j - 2)
                        if not begun(b):
                            if (j, a) == (0, 0):
                                route_weights()
                            if (j, a) == (0, 5):
                                route_places()
                            if j == 1 and a in (1, 5):
                                route_slots(a // 4)
                        if begun(b):
                            if (j, a) == (2, 1):
                                finish_recip(b - 1)
                            if (j, a) == (3, 7):
                                finish_norm(b - 1)
                            if (j, a) == (3, 11):
                                finish_add(b - 1)
                        if experts:
                            if (j, a) == (1, 7):
                                weigh(e, 0)
                            if (j, a) == (2, 4):
                                expert_out(e, 0)
                            if (j, a) == (2, 7):
                                weigh(e + 1, 1)
                            if (j, a) == (3, 4):
                                expert_out(e + 1, 1)

            router(1)
            for w in range(2):
                for k in range(2):
                    ropes(0, w, k, bank_a[1 + k])
                split(0, w, 0)
            for k in range(1, 3):
                for w in range(2):
                    split(0, w, k)
            with dve.Fori(2, B - 2) as b:
                router(b)
            router(B - 2)
            router(B - 1)
            for a in range(3):
                rowmax(0, 0, a)
            top_two(B - 1)
            v.tensor_tensor(picked[:], hot[0][:], hot[1][:], ALU.add).then_inc(s["picked_ready"], 1)
            for a in range(3, NA):
                rowmax(0, 0, a)
            neg_max(0, 0)

            for a in range(NA):
                rowmax(0, 1, a)
            sequences(body, dve)
            for j in range(2, QUADS):
                if j == 3:
                    add_ffn(B - 2)
                    add_ffn(B - 1)
                scale_o(j)
            finish_add(B - 1)

        @block.gpsimd
        def _(pool):
            p = nc.gpsimd

            def keep_xn(b):
                pool.wait_ge(s["var_ready"], 3 * b + 3)
                at_least(pool, s["xn_ready"], b)
                p.tensor_tensor(rstd[:], vpe[:], nhalf[:], ALU.pow).then_inc(s["rstd_ready"], 1)
                pool.wait_ge(s["xn_ready"], b + 1)
                p.tensor_copy(xrow[:, bass.ds(b * TS, TS), 0:C], xn[:]).then_inc(s["xn_kept"], 1)

            pool.wait_ge(s["sums_init"], 1)
            keep_xn(0)
            for b in range(1, 5):
                pool.wait_ge(s["xn_kept"], b)
                half = slice(0, 2) if b % 2 else slice(2, 4)
                if b < 3:
                    p.memset(K[64:KROWS, half], 1.0).then_inc(s["rows_set"], 1)
                else:
                    p.memset(Q[64:KROWS, half], 0.0).then_inc(s["rows_set"], 1)
                pool.wait_ge(s["rows_set"], b)
                keep_xn(b)
            p.memset(vaug[:], 1.0).then_inc(s["ones_set"], 1)
            with pool.Fori(5, B) as b:
                keep_xn(b)

            def scatter(i):
                if i == 0:
                    pool.wait_ge(s["slots_ready"], 2)
                    pool.wait_ge(s["slots_zeroed"], 16 * E)
                    pool.wait_ge(s["rows_ready"], 16)
                k, t = SCATTERS[i]
                p.indirect_dma_start(slot_rows, bass.IndirectOffsetOnAxis(ap=slot[:, k, t:t + 1], axis=0),
                                     xrow[:, t, :], None, bounds_check=E * CAP - 1, oob_is_err=False).then_inc(s["scattered"], 16)

            def diagonal(cols, unit):
                if len(unit) == 1:
                    return cols[:, 0:P], [[1, P]]
                gap_tiles = unit[1][2] // P
                return cols.rearrange("p (k n) -> p k n", k=TS)[:, 0:gap_tiles + 1:gap_tiles, :], [[0, 2], [1, P]]

            def expert_back(e, i):
                pool.wait_ge(s["ffn_zeroed"], 16 * (B + 1))
                pool.wait_ge(s["eo_ready_out"], e + 1)
                wait_first(pool, s["pool_passed"], s["eo_added"], 16 * TS * e)
                for t in range(TS):
                    p.indirect_dma_start(ffn_rows, bass.IndirectOffsetOnAxis(ap=back[:, i, t:t + 1], axis=0),
                                         eo[:, t * C:(t + 1) * C], None, bounds_check=N + CAP - 1, oob_is_err=True,
                                         compute_op=ALU.add).then_inc(s["eo_added"], 16)

            def body(b, experts):
                e = 2 * (b - EXPERT_FROM)
                for j in range(QUADS):
                    g = QUADS * b + j
                    for u, unit in enumerate(UNITS):
                        n = NU * g + u
                        wait_first(pool, s["pool_passed"], s["exp_done"], n + 1)
                        tile, pattern = diagonal(probs[:, j % 2, u * 512:(u + 1) * 512], unit)
                        p.affine_select(out=tile, in_=tile, compare_op=ALU.is_ge, fill=0.0, base=0, pattern=pattern,
                                        channel_multiplier=-1).then_inc(s["probs_masked"], 1)
                        if u == 8:
                            at_least(pool, s["pv_done"], QUADS * (b - 1) + j + 1)
                            wait_first(pool, s["pool_passed"], s["v_copied"], b + 1)
                            p.tensor_scalar(vaug[:, j, :, :, 0:DK], vstage[:, :, 4 * j:4 * j + 4, :], 1.0, 0.0,
                                            ALU.mult, ALU.add).then_inc(s["vaug_ready"], 1)
                        if isinstance(b, int) and b < EXPERT_FROM and n >= SCATTER_FROM:
                            m = n - SCATTER_FROM
                            for i in range(len(SCATTERS) * m // SPREAD, len(SCATTERS) * (m + 1) // SPREAD):
                                scatter(i)
                        if experts and (j, u) == (2, 5):
                            expert_back(e, 0)
                        if experts and (j, u) == (3, 5):
                            expert_back(e + 1, 1)

            pool.wait_ge(s["ones_set"], 1)
            sequences(body, pool)

        @block.scalar
        def _(act):
            a = nc.scalar
            act.dma_start(ident[:], ident_in).then_inc(s["ident_loaded"], 16)
            act.dma_start(bias_rows[0:HJ, :], rb1.rearrange("(j p) -> j p", p=P)).then_inc(s["bias_loaded"], 16)
            act.dma_start(bias_rows[HJ:, :], eb1.rearrange("e (j p) -> (e j) p", p=P)).then_inc(s["bias_loaded"], 16)
            act.dma_start(w1r, rw1).then_inc(s["router_loaded"], 16)
            act.wait_ge(s["w2r_zero"], 1)
            act.dma_start(w2r[:, :, 0:E], rw2.rearrange("(j p) e -> p j e", p=P)).then_inc(s["router_loaded"], 16)
            act.dma_start(b2r[:], rb2.rearrange("(o e) -> o e", o=1).broadcast_to([P, E])).then_inc(s["router_loaded"], 16)
            act.dma_start(sel[:], sel_in).then_inc(s["router_loaded"], 16)

            def copy_xnT(b):
                act.wait_ge(s["xnT_ready"], b + 1)
                a.copy(xnT[:, bass.ds(b * S, S)], bank_a[0][:]).then_inc(s["xnT_copied"], 1)

            act.wait_ge(s["biases_ready"], 1)
            a.copy(biases[:], bank_misc[:, 0:HJ * (E + 1)]).then_inc(s["biases_copied"], 1)
            copy_xnT(0)
            act.wait_ge(s["biases_copied"], 1)

            def router(b):
                for h in range(HJ):
                    act.wait_ge(s["hid_ready"], HJ * b + h + 1)
                    if h == 0:
                        at_least(act, s["lgT_ready"], b)
                    a.activation(hid[:, h, :], bank_b[h % 2][:], ACT.Relu, bias=biases[:, h:h + 1]).then_inc(s["hid_relu"], 1)
                if not is_last(b):
                    copy_xnT(b + 1)
                act.wait_ge(s["lgT_ready"], b + 1)
                at_least(act, s["lg_ready"], b)
                a.copy(lgT[:], bank_o[:]).then_inc(s["lgT_copied"], 1)

            def part(b, w, k):
                i = 2 * b + w
                if k == 0:
                    act.wait_ge(s["rope_sum"], i + 1)
                    at_least(act, s["qk_stored"], 96 * b)
                    a.copy(parts[:, w, 0, :], qk[:, w, :]).then_inc(s["part1"], 1)
                else:
                    act.wait_ge(s["rest1"], i + 1)
                    a.copy(parts[:, w, 1, :], qk[:, w, :]).then_inc(s["part2"], 1)

            def evict_o(b, j):
                act.wait_ge(s["pv_done"], QUADS * b + j + 1)
                if is_last(b) and j > 1:
                    act.wait_ge(s["o_turned"], j - 1)
                else:
                    at_least(act, o_stored[j % 2], 16 * (2 * b + j // 2))
                a.copy(osb[:, j % 2, :], bank_o[:]).then_inc(s["o_copied"], 1)

            def store_max(b, j):
                g = QUADS * b + j
                act.wait_ge(s["negm_ready"], 2 * g + 2)
                act.dma_start(m_dram[bass.ds(g * 16, 16), :], negm[:].rearrange("p k q -> p (k q)")).then_inc(s["m_stored"], 16)

            def load_max(b, j):
                g = QUADS * b + j
                act.wait_ge(s["m_stored"], 16 * g + 16)
                act.wait_ge(s["rowmax_done"], 16 * (g + 1))
                act.dma_start(Q[MROW:MROW + 2, j].rearrange("p h (t q) -> p (h t) q", q=P),
                              m_dram[bass.ds(g * 16, 16), :].rearrange("a (k q) -> k a q", k=2)).then_inc(m_loaded[j], 16)

            def turn_rows(e):
                act.wait_ge(s["dT_ready"], e + 1)
                at_least(act, s["eh_ready"], HJ * e)
                a.copy(dspT[:], bank_misc[:]).then_inc(s["dT_copied"], 1)

            def relu(e, h):
                act.wait_ge(s["eh_ready"], HJ * e + h + 1)
                if h == 0:
                    at_least(act, s["eo_ready"], e)
                a.activation(hid[:, h, :], (bank_proj, bank_misc)[h % 2][:], ACT.Relu,
                             bias=biases[:, bass.ds(HJ * e + HJ + h, 1)]).then_inc(s["eh_relu"], 1)

            def body(b, experts):
                last = is_last(b)
                e = 2 * (b - EXPERT_FROM)
                for j in range(QUADS):
                    g = QUADS * b + j
                    for u in range(NU):
                        n = NU * g + u
                        act.wait_ge(s["scores_ready"], n + 1)
                        if u == 0:
                            at_least(act, s["pv_done"], g - 1)
                        a.activation(probs[:, j % 2, u * 512:(u + 1) * 512], bank_b[u % 2][:], ACT.Exp, scale=SCALE).then_inc(s["exp_done"], 1)
                        if experts and j in (1, 2):
                            if u == 4:
                                turn_rows(e + j - 1)
                            if u in (5, 6, 7, 8):
                                relu(e + j - 1, (5, 6, 7, 8).index(u))
                        if u in (3, 6):
                            step = store_max if u == 3 else load_max
                            if j < 3:
                                step(b, j + 1)
                            elif not last:
                                step(b + 1, 0)
                        if j == 0 and u == 7:
                            act.wait_ge(s["v_ready"], b + 1)
                            at_least(act, s["vaug_ready"], QUADS * b)
                            a.copy(vstage[:].rearrange("p t h d -> p (t h d)"), bank_misc[:]).then_inc(s["v_copied"], 1)
                        if not last:
                            if j == 0 and u in (4, 6):
                                part(b + 1, 0, (u - 4) // 2)
                            if j == 0 and u == 8:
                                part(b + 1, 1, 0)
                            if j == 1 and u == 0:
                                part(b + 1, 1, 1)
                        if u == 9:
                            if j > 0:
                                evict_o(b, j - 1)
                            elif begun(b):
                                evict_o(b - 1, 3)

            router(0)
            router(1)
            for k in range(2):
                for w in range(2):
                    part(0, w, k)
            with act.Fori(2, B - 1) as b:
                router(b)
            router(B - 1)
            act.wait_ge(s["topped"], TOPS * B)
            a.activation(small[0][:], gap[:], ACT.Exp).then_inc(s["gap_exp"], 1)
            act.wait_ge(s["route_loaded"], 16 * 4)
            act.wait_ge(s["xn_kept"], B)
            a.copy(xrow[:, :, TOKEN], small[7][:]).then_inc(s["rows_ready"], 16)
            act.wait_ge(s["counts_ready"], 1)
            a.copy(within[:], bank_proj[:, 0:NT * E])
            a.copy(totals[:], bank_proj[:, NT * E:2 * NT * E]).then_inc(s["counts_copied"], 1)
            store_max(0, 0)
            load_max(0, 0)
            sequences(body, act)
            evict_o(B - 1, 3)
            act.wait_ge(s["out_ready"], B - 1)
            act.wait_ge(s["ot_ready"], 1)
            a.copy(oT[:], bank_proj[:]).then_inc(s["ot_copied"], 1)

        @block.tensor
        def _(pe):
            t = nc.tensor

            def turn_xn(b):
                pe.wait_ge(s["xn_ready"], b + 1)
                at_least(pe, s["xnT_copied"], b)
                for i in range(TS):
                    ins = t.transpose(bank_a[0][:, i * P:(i + 1) * P], xn[:, i, :], ident[:])
                ins.then_inc(s["xnT_ready"], 1)

            def sum_logits(b):
                pe.wait_ge(s["lgT_copied"], b + 1)
                at_least(pe, s["topped"], TOPS * b)
                for i in range(TS):
                    ins = t.matmul(bank_proj[:, i * E:(i + 1) * E], lgT[:, i * P:(i + 1) * P], sel[:], start=True, stop=True)
                ins.then_inc(s["lg_ready"], 1)

            def router(b):
                for h in range(HJ):
                    if h == 0:
                        pe.wait_ge(s["xnT_copied"], b + 1)
                    at_least(pe, s["hid_relu"], HJ * b + h - 1)
                    t.matmul(bank_b[h % 2][:], w1r[:, h * P:(h + 1) * P], xnT[:, bass.ds(b * S, S)], start=True, stop=True).then_inc(s["hid_ready"], 1)
                    if h == 1 and begun(b):
                        sum_logits(b - 1)
                if not is_last(b):
                    turn_xn(b + 1)
                pe.wait_ge(s["hid_relu"], HJ * b + HJ)
                at_least(pe, s["lgT_copied"], b)
                for h in range(HJ):
                    ins = t.matmul(bank_o[32 * h:32 * h + 32, :], w2r[:, h, :], hid[:, h, :], start=True, stop=True)
                ins.then_inc(s["lgT_ready"], 1)

            pe.wait_ge(s["ident_loaded"], 16)
            pe.wait_ge(s["bias_loaded"], 32)
            t.transpose(bank_misc[:, 0:HJ * (E + 1)], bias_rows[:], ident[0:HJ * (E + 1), 0:HJ * (E + 1)]).then_inc(s["biases_ready"], 1)
            turn_xn(0)
            pe.wait_ge(s["router_loaded"], 16 * 4)
            router(0)
            router(1)

            def project(b, w, k, bank=bank_proj, banks=1):
                at_least(pe, s["rope_mul"], 4 * b + 2 * w + k + 1 - banks)
                if w == 0 and k == 0:
                    at_least(pe, s["eo_biased"], 2 * (b - 1 - EXPERT_FROM))
                t.matmul(bank[:], ((wq, wqr), (wk, wkr))[w][k][:], xnT[:, bass.ds(b * S, S)], start=True, stop=True).then_inc(s["proj_ready"], 1)

            def project_v(b):
                pe.wait_ge(s["xv_loaded"], 16 * b + 16)
                pe.wait_ge(s["negm_ready"], 2 * (QUADS * b + 2))
                for i in range(TS):
                    ins = t.matmul(bank_misc[:, i * P:(i + 1) * P], xv[:, i * P:(i + 1) * P], wv[:], start=True, stop=True)
                ins.then_inc(s["v_ready"], 1)

            def scores_a(b, j, a):
                h, tiles = AUNITS[a]
                g = QUADS * b + j
                before_it = 16 * g + 4 * (a // 3) + (0, 2, 3)[a % 3]
                at_least(pe, s["rowmax_done"], before_it - 4 + (2, 1, 1)[a % 3])
                if a == 0:
                    pe.wait_ge(slot_loaded[j], 48 * (b + 1))
                for qt, c in tiles:
                    ins = t.matmul(bank_a[a % 3][:, c:c + P * (qt + 1)], Q[0:KROWS, j, h, qt * P:(qt + 1) * P],
                                   K[0:KROWS, j, h, 0:P * (qt + 1)], start=True, stop=True)
                ins.then_inc(s["a_ready"], 1)

            def turn_max(b, j):
                g = QUADS * b + j
                pe.wait_ge(s["rowmax_done"], 16 * (g + 1))
                if j == 2:
                    pe.wait_ge(s["v_copied"], b + 1)
                if j == 1:
                    at_least(pe, s["res_added"], b - 1)
                t.transpose(bank_misc[0:16, 0:P], rmax[:, j % 2, :], ident[:]).then_inc(s["mt_ready"], 1)

            def scores_b(b, j, u):
                n = NU * (QUADS * b + j) + u
                at_least(pe, s["exp_done"], n - 1)
                if u == 0:
                    pe.wait_ge(m_loaded[j], 16 * (b + 1))
                for h, kt, c, w in UNITS[u]:
                    ins = t.matmul(bank_b[u % 2][:, c:c + w], K[0:KROWS, j, h, kt * P:(kt + 1) * P], Q[0:KROWS, j, h, kt * P:S],
                                   start=True, stop=True)
                ins.then_inc(s["scores_ready"], 1)

            def weigh_v(b, j, kt):
                g = QUADS * b + j
                if kt == 0:
                    pe.wait_ge(s["probs_masked"], NU * (g + 1))
                    pe.wait_ge(s["vaug_ready"], g + 1)
                    at_least(pe, s["o_copied"], g)
                for h in range(4):
                    at, w = PIECE[h, kt]
                    ins = t.matmul(bank_o[VW * h:VW * h + VW, kt * P:S], vaug[:, j, kt, h, :], probs[:, j % 2, at:at + w],
                                   start=(kt == 0), stop=(kt == TS - 1), skip_group_check=True)
                if kt == TS - 1:
                    ins.then_inc(s["pv_done"], 1)

            def turn_o(j):
                pe.wait_ge(s["o_copied"], QUADS * (B - 1) + j + 1)
                pe.wait_ge(s["rowmax_done"], 16 * QUADS * B)
                at_least(pe, s["o_scaled"], j - 2)
                for i in range(TS):
                    ins = t.transpose(bank_a[j % 3][:, i * P:(i + 1) * P], osb[:, j % 2, i * P:(i + 1) * P], ident[:])
                ins.then_inc(s["o_turned"], 1)

            def project_o(b, maxima):
                if is_last(b):
                    pe.wait_ge(s["ot_copied"], 1)
                else:
                    pe.wait_ge(s["on_ready"], b + 1)
                pe.wait_ge(s["negm_ready"], 2 * maxima)
                for i in range(TS):
                    ins = t.matmul(bank_misc[:, i * P:(i + 1) * P], oT[:, i * P:(i + 1) * P], wo[:], start=True, stop=True)
                ins.then_inc(s["out_ready"], 1)

            def expert_turn(e, i, maxima):
                pe.wait_ge(ew_loaded[i], 64 + 32 * (e - i))
                pe.wait_ge(s["negm_ready"], 2 * maxima)
                for k in range(TS):
                    ins = t.transpose(bank_misc[:, k * P:(k + 1) * P], dsp[:, i, k, 0:C], ident[:])
                ins.then_inc(s["dT_ready"], 1)

            def expert_hidden(e, i, h, maxima):
                if h == 0:
                    pe.wait_ge(s["dT_copied"], e + 1)
                    at_least(pe, s["eo_biased"], e)
                elif h == 1:
                    pe.wait_ge(s["negm_ready"], 2 * maxima)
                else:
                    pe.wait_ge(s["eh_relu"], HJ * e + h - 1)
                t.matmul((bank_proj, bank_misc)[h % 2][:], w1s[:, i, h * P:(h + 1) * P], dspT[:], start=True, stop=True).then_inc(s["eh_ready"], 1)

            def expert_result(e, i, k):
                if k == TS - 1:
                    pe.wait_ge(s["eh_relu"], HJ * e + HJ)
                for h in range(HJ):
                    ins = t.matmul(bank_proj[:, k * P:(k + 1) * P], hid[:, h, k * P:(k + 1) * P], w2s[:, i, h, :],
                                   start=(h == 0), stop=(h == HJ - 1))
                if k == TS - 2:
                    ins.then_inc(s["eo_ready"], 1)

            def body(b, experts):
                last = is_last(b)
                e = 2 * (b - EXPERT_FROM)
                for j in range(QUADS):
                    done = 0
                    turned = QUADS * b + j + 2
                    for u in range(NU):
                        if experts and j in (1, 2) and u in (5, 6, 7, 8):
                            expert_hidden(e + j - 1, j - 1, (5, 6, 7, 8).index(u), turned)
                        if experts and j in (2, 3) and 1 <= u < 4:
                            if u == 1:
                                expert_result(e + j - 2, j - 2, 3)
                            expert_result(e + j - 2, j - 2, u - 1)
                        if j == 0 and not last and u in (0, 3, 6, 8):
                            i = (0, 3, 6, 8).index(u)
                            project(b + 1, i // 2, i % 2)
                        scores_b(b, j, u)
                        if u == 1:
                            if experts and j in (2, 3):
                                pe.wait_ge(s["eh_relu"], HJ * (e + j - 1))
                            if j < 3:
                                turn_max(b, j + 1)
                            elif not last:
                                turn_max(b + 1, 0)
                        for _ in range(A_BESIDE[u]):
                            if j < 2:
                                scores_a(b, j + 2, done)
                            elif not last:
                                scores_a(b + 1, j - 2, done)
                            done += 1
                        if experts and j in (1, 2) and u == 3:
                            expert_turn(e + j - 1, j - 1, turned)
                        if j == 0 and u == 6:
                            project_v(b)
                        if u in (2, 4, 6, 8):
                            if j > 0:
                                weigh_v(b, j - 1, u // 2 - 1)
                            elif begun(b):
                                weigh_v(b - 1, 3, u // 2 - 1)
                        if last and j > 1 and u == 0:
                            turn_o(j - 2)
                        if j == 3 and u == 9 and begun(b):
                            project_o(b - 1, QUADS * (b + 1) + (0 if last else 1))

            pe.wait_ge(s["attn_loaded"], 16 * 7)
            pe.wait_ge(s["rotated"], 4)
            for i in range(4):
                project(0, i // 2, i % 2, bank_a[1 + i % 2], 2)
            with pe.Fori(2, B - 1) as b:
                router(b)
            router(B - 1)
            pe.wait_ge(s["xnT_copied"], B)
            pe.wait_ge(s["rope_mul"], 4)
            for a in range(3):
                scores_a(0, 0, a)
            sum_logits(B - 1)
            for a in range(3, NA):
                scores_a(0, 0, a)
                if a == 6:
                    pe.wait_ge(s["route_loaded"], 16 * 4)
                    pe.wait_ge(s["sums_init"], 2)
                    pe.wait_ge(s["picked_ready"], 1)
                    t.matmul(bank_proj[:, 0:NT * E], tri[:], picked[:], start=True, stop=True)
                    t.matmul(bank_proj[:, NT * E:2 * NT * E], ones[:], picked[:], start=True, stop=True).then_inc(s["counts_ready"], 1)
            pe.wait_ge(s["biases_copied"], 1)
            turn_max(0, 0)
            for a in range(NA):
                scores_a(0, 1, a)
            pe.wait_ge(s["counts_copied"], 1)
            sequences(body, pe)
            for kt in range(TS):
                weigh_v(B - 1, 3, kt)
            turn_o(2)
            turn_o(3)
            pe.wait_ge(s["o_scaled"], QUADS)
            for i in range(TS):
                ins = t.transpose(bank_proj[:, i * P:(i + 1) * P], otok[:, i * P:(i + 1) * P], ident[:])
            ins.then_inc(s["ot_ready"], 1)
            pe.wait_ge(s["res_added"], B - 1)
            project_o(B - 1, QUADS * B)


def constants(B, S, DK, E, CAP):
    import numpy as np
    f = np.float32
    N = B * S
    pos = np.arange(S, dtype=f)
    inv = (f(1.0) / np.power(f(10000.0), np.arange(0, DK, 2, dtype=f) / f(DK))).astype(f)
    angles = np.outer(pos, inv).astype(f)
    cos = np.repeat(np.cos(angles), 2, axis=-1).astype(f)
    sin = np.repeat(np.sin(angles), 2, axis=-1).astype(f)
    q = np.arange(P)
    amask = np.zeros((P, S), f)
    amask[:, S - P:] = np.where(q[None, :] <= q[:, None], 0.0, -BIG)
    sel = np.zeros((P, E), f)
    for h in range(4):
        sel[32 * h + np.arange(E), np.arange(E)] = 1.0
    erow = np.concatenate([E - np.arange(E), CAP * np.arange(E)]).astype(f)
    token = (q[:, None] + P * np.arange(N // P)[None, :]).astype(f)
    return {
        "ident": np.eye(P, dtype=f),
        "cosT": np.ascontiguousarray(np.tile(cos.T, (HEADS, 1))),
        "sinT": np.ascontiguousarray(np.tile(sin.T, (HEADS, 1))),
        "amask": amask,
        "tri": (q[:, None] <= q[None, :]).astype(f),
        "sel": sel,
        "erow": np.ascontiguousarray(np.tile(erow, (P, 1))),
        "token": np.ascontiguousarray(token + f(1.0)),
        "trash": np.ascontiguousarray(token[:, 0:S // P] + f(N + 1)),
        "zeros": np.zeros((2, 2 * S), f),
    }


_INS = ["L0_attn_x", "L0_attn_Wq", "L0_attn_Wk", "L0_attn_Wv", "L0_attn_Wo", "L0_ffn_rw1", "L0_ffn_rb1",
        "L0_ffn_rw2", "L0_ffn_rb2", "L0_ffn_ew1", "L0_ffn_eb1", "L0_ffn_ew2", "L0_ffn_eb2"]


def kernel(**inputs):
    import numpy as _np
    import concourse.bacc as _bacc
    from concourse import mybir as _mybir
    from concourse.bass_utils import run_bass_kernel_spmd as _run

    nc = _bacc.Bacc("TRN2", target_bir_lowering=False, num_devices=1)
    B, S, C = inputs["L0_attn_x"].shape
    E = inputs["L0_ffn_ew1"].shape[0]
    arrays, args = {}, []
    named = {n: _np.ascontiguousarray(inputs[n]) for n in _INS}
    named.update(constants(B, S, C // HEADS, E, S))
    for name, a in named.items():
        arrays[f"in_{name}_dram"] = a
        args.append(nc.dram_tensor(f"in_{name}_dram", a.shape, _mybir.dt.from_np(a.dtype), kind="ExternalInput").ap())
    args.append(nc.dram_tensor("out_0_dram", (B, S, C), F32, kind="ExternalOutput").ap())
    build(nc, *args)
    r = _run(nc, [arrays], core_ids=[0])
    return r.results[0]["out_0_dram"]
```
